# Optimizing a Trainium2 kernel written in Bass

```python
import numpy as np
import jax
import jax.numpy as jnp

def _softmax(x, axis=-1):
    return jax.nn.softmax(x, axis=axis)

def _gelu(x):
    return jax.nn.gelu(x, approximate=True)

def _silu(x):
    return jax.nn.silu(x)

def _sigmoid(x):
    return jax.nn.sigmoid(x)

def _layernorm(x, axis=-1, eps=1e-05):
    m = jnp.mean(x, axis=axis, keepdims=True)
    v = jnp.var(x, axis=axis, keepdims=True)
    return (x - m) / jnp.sqrt(v + eps)

def _scatter_add(tgt, idx, src, axis=0):
    return tgt.at[idx].add(src)

def _segment_sum(src, seg, n):
    return jax.ops.segment_sum(src, seg, n)
kernel_name = 'mk_adaln_attn_ffn_d1_seqx_r8_4dcc5e'

def setup_inputs(seed: int=0):
    np.random.seed(seed)
    _w = jnp.asarray

    def _rec_inputs():
        import jax
        import jax.numpy as jnp
        _rk = jax.random.key(seed)
        x = -0.000125 + 0.9999 * jax.random.normal(jax.random.fold_in(_rk, 1), (2, 512, 128), jnp.float32)
        _lenS = 512 - jax.random.randint(jax.random.fold_in(_rk, 7), (2,), 0, max(1, 512 // 4) + 1, jnp.int32)
        _lenS2 = 512 - jax.random.randint(jax.random.fold_in(_rk, 8), (2,), 0, max(1, 512 // 4) + 1, jnp.int32)
        cond_1024 = -0.00493535 + 1.00056 * jax.random.normal(jax.random.fold_in(_rk, 11), (2, 128), jnp.float32)
        return (x, cond_1024)
    x, cond_1024 = _rec_inputs()

    def _L0_cond_setup():
        import jax, jax.numpy as jnp
        import numpy as np
        import math
        D = 128
        H = 128
        key = jax.random.key(seed)
        k1, k2, k3, k4 = jax.random.split(key, 4)
        x = jax.random.normal(k1, (64, 64, D), dtype=jnp.float32)
        h0 = jax.random.normal(k2, (64, H), dtype=jnp.float32)
        Wx = jax.random.normal(k3, (D, 4 * H), dtype=jnp.float32) / math.sqrt(D)
        Wh = jax.random.normal(k4, (H, 4 * H), dtype=jnp.float32) / math.sqrt(H)
        b = jnp.zeros((4 * H,), dtype=jnp.float32)
        return {'x': x, 'h0': h0, 'Wx': Wx, 'Wh': Wh, 'b': b}
    _L0_cond_all = _L0_cond_setup()
    _L0_cond_in = {k: v for k, v in _L0_cond_all.items() if k in ('Wx', 'Wh', 'b')}
    del _L0_cond_all

    def _L0_attn_setup():
        import jax, jax.numpy as jnp
        import numpy as np
        N_EMBD = 128
        BLOCK_SIZE = 256
        ATTN_SPAN = 32
        LN_EPS = 1e-05

        def _band_mask(T, span, dtype):
            ones = jnp.ones((T, T), dtype=dtype)
            return jnp.tril(ones, 0) * (1.0 - jnp.tril(ones, -span))

        def _layer_norm(h, w, b):
            mu = jnp.mean(h, axis=-1, keepdims=True)
            var = jnp.var(h, axis=-1, keepdims=True)
            return (h - mu) * jax.lax.rsqrt(var + LN_EPS) * w + b
        key = jax.random.key(seed)
        k_x, k_w, k_b, k_lw = jax.random.split(key, 4)
        B, T, C = (4, BLOCK_SIZE, N_EMBD)
        x = jax.random.normal(k_x, (B, T, C), dtype=jnp.float32)
        lim = 1.0 / np.sqrt(C)
        W_qkv = jax.random.uniform(k_w, (C, 3 * C), minval=-lim, maxval=lim, dtype=jnp.float32)
        b_qkv = jax.random.uniform(k_b, (3 * C,), minval=-lim, maxval=lim, dtype=jnp.float32)
        ln_w = jnp.ones((C,), dtype=jnp.float32)
        ln_b = jnp.zeros((C,), dtype=jnp.float32)
        return {'x': x, 'W_qkv': W_qkv, 'b_qkv': b_qkv, 'ln_w': ln_w, 'ln_b': ln_b}
    _L0_attn_all = _L0_attn_setup()
    _L0_attn_in = {k: v for k, v in _L0_attn_all.items() if k in ('W_qkv', 'b_qkv', 'ln_w', 'ln_b')}
    del _L0_attn_all

    def _L0_cond2_setup():
        import jax, jax.numpy as jnp
        import numpy as np
        B, T, D_IN, V_IN, E = (64, 128, 128, 128, 128)
        key = jax.random.key(seed)
        ks = jax.random.split(key, 16)
        s = 0.01
        return {'video': jax.random.normal(ks[0], (B, V_IN), jnp.float32), 'seq': jax.random.normal(ks[1], (B, T, D_IN), jnp.float32), 'W_z': jax.random.normal(ks[2], (D_IN, E), jnp.float32) * s, 'U_z': jax.random.normal(ks[3], (E, E), jnp.float32) * s, 'C_z': jax.random.normal(ks[4], (V_IN, E), jnp.float32) * s, 'b_z': jnp.zeros((E,), jnp.float32), 'W_r': jax.random.normal(ks[5], (D_IN, E), jnp.float32) * s, 'U_r': jax.random.normal(ks[6], (E, E), jnp.float32) * s, 'C_r': jax.random.normal(ks[7], (V_IN, E), jnp.float32) * s, 'b_r': jnp.zeros((E,), jnp.float32), 'W': jax.random.normal(ks[8], (D_IN, E), jnp.float32) * s, 'U': jax.random.normal(ks[9], (E, E), jnp.float32) * s, 'C': jax.random.normal(ks[10], (V_IN, E), jnp.float32) * s, 'b': jnp.zeros((E,), jnp.float32)}
    _L0_cond2_all = _L0_cond2_setup()
    _L0_cond2_in = {k: v for k, v in _L0_cond2_all.items() if k in ('W_z', 'U_z', 'C_z', 'b_z', 'W_r', 'U_r', 'C_r', 'b_r', 'W', 'U', 'C', 'b')}
    del _L0_cond2_all

    def _L0_ffn_setup():
        import jax, jax.numpy as jnp
        import numpy as np
        B, T, D, H, E = (4, 256, 128, 256, 8)
        TOP_K = int(E * 0.25)
        key = jax.random.key(seed)
        ks = jax.random.split(key, 6)
        x = jax.random.normal(ks[0], (B, T, D), dtype=jnp.float32)
        gate = jax.random.normal(ks[1], (D, E), dtype=jnp.float32)
        W1 = jax.random.normal(ks[2], (E, D, H), dtype=jnp.float32) * D ** (-0.5)
        b1 = jnp.zeros((E, H), dtype=jnp.float32)
        W2 = jax.random.normal(ks[3], (E, H, D), dtype=jnp.float32) * H ** (-0.5)
        b2 = jnp.zeros((E, D), dtype=jnp.float32)
        return {'x': x, 'gate': gate, 'W1': W1, 'b1': b1, 'W2': W2, 'b2': b2}
    _L0_ffn_all = _L0_ffn_setup()
    _L0_ffn_in = {k: v for k, v in _L0_ffn_all.items() if k in ('gate', 'W1', 'b1', 'W2', 'b2')}
    del _L0_ffn_all
    return {'x': x, 'cond_1024': cond_1024, 'L0_cond_Wx': _L0_cond_in['Wx'], 'L0_cond_Wh': _L0_cond_in['Wh'], 'L0_cond_b': _L0_cond_in['b'], 'L0_attn_W_qkv': _L0_attn_in['W_qkv'], 'L0_attn_b_qkv': _L0_attn_in['b_qkv'], 'L0_attn_ln_w': _L0_attn_in['ln_w'], 'L0_attn_ln_b': _L0_attn_in['ln_b'], 'L0_cond2_W_z': _L0_cond2_in['W_z'], 'L0_cond2_U_z': _L0_cond2_in['U_z'], 'L0_cond2_C_z': _L0_cond2_in['C_z'], 'L0_cond2_b_z': _L0_cond2_in['b_z'], 'L0_cond2_W_r': _L0_cond2_in['W_r'], 'L0_cond2_U_r': _L0_cond2_in['U_r'], 'L0_cond2_C_r': _L0_cond2_in['C_r'], 'L0_cond2_b_r': _L0_cond2_in['b_r'], 'L0_cond2_W': _L0_cond2_in['W'], 'L0_cond2_U': _L0_cond2_in['U'], 'L0_cond2_C': _L0_cond2_in['C'], 'L0_cond2_b': _L0_cond2_in['b'], 'L0_ffn_gate': _L0_ffn_in['gate'], 'L0_ffn_W1': _L0_ffn_in['W1'], 'L0_ffn_b1': _L0_ffn_in['b1'], 'L0_ffn_W2': _L0_ffn_in['W2'], 'L0_ffn_b2': _L0_ffn_in['b2']}

def reference(x, cond_1024, L0_cond_Wx, L0_cond_Wh, L0_cond_b, L0_attn_W_qkv, L0_attn_b_qkv, L0_attn_ln_w, L0_attn_ln_b, L0_cond2_W_z, L0_cond2_U_z, L0_cond2_C_z, L0_cond2_b_z, L0_cond2_W_r, L0_cond2_U_r, L0_cond2_C_r, L0_cond2_b_r, L0_cond2_W, L0_cond2_U, L0_cond2_C, L0_cond2_b, L0_ffn_gate, L0_ffn_W1, L0_ffn_b1, L0_ffn_W2, L0_ffn_b2):
    import jax
    import jax.numpy as jnp

    def _L0_cond_ref(x, h0, Wx, Wh, b):
        import jax, jax.numpy as jnp
        import numpy as np
        import math
        D = 128
        H = 128
        xz = jnp.einsum('ntd,dk->ntk', x, Wx) + b
        c0 = jnp.zeros_like(h0)

        def step(carry, xz_t):
            prev_h, prev_c = carry
            z = xz_t + prev_h @ Wh
            ai, af, ao, ag = jnp.split(z, 4, axis=1)
            i = jax.nn.sigmoid(ai)
            f = jax.nn.sigmoid(af)
            o = jax.nn.sigmoid(ao)
            g = jnp.tanh(ag)
            next_c = f * prev_c + i * g
            next_h = o * jnp.tanh(next_c)
            return ((next_h, next_c), next_h)
        _, hs = jax.lax.scan(step, (h0, c0), jnp.swapaxes(xz, 0, 1))
        return jnp.swapaxes(hs, 0, 1)

    def _L0_attn_ref(x, W_qkv, b_qkv, ln_w, ln_b):
        import jax, jax.numpy as jnp
        import numpy as np
        N_EMBD = 128
        BLOCK_SIZE = 256
        ATTN_SPAN = 32
        LN_EPS = 1e-05

        def _band_mask(T, span, dtype):
            ones = jnp.ones((T, T), dtype=dtype)
            return jnp.tril(ones, 0) * (1.0 - jnp.tril(ones, -span))

        def _layer_norm(h, w, b):
            mu = jnp.mean(h, axis=-1, keepdims=True)
            var = jnp.var(h, axis=-1, keepdims=True)
            return (h - mu) * jax.lax.rsqrt(var + LN_EPS) * w + b
        B, T, C = x.shape
        qkv = x @ W_qkv + b_qkv
        q, k, v = jnp.split(qkv, 3, axis=-1)
        scale = np.sqrt(C * ATTN_SPAN).astype(np.float32)
        scores = jnp.einsum('bid,bjd->bij', q, k) / scale
        scores = scores * _band_mask(T, ATTN_SPAN, x.dtype)[None, :, :]
        out = jnp.einsum('bij,bjd->bid', scores, v)
        return _layer_norm(out, ln_w, ln_b)

    def _L0_cond2_ref(video, seq, W_z, U_z, C_z, b_z, W_r, U_r, C_r, b_r, W, U, C, b):
        import jax, jax.numpy as jnp
        import numpy as np
        B, T, D_IN, V_IN, E = (64, 128, 128, 128, 128)
        vz = video @ C_z + b_z
        vr = video @ C_r + b_r
        vh = video @ C + b
        xz = jnp.einsum('btd,de->bte', seq, W_z)
        xr = jnp.einsum('btd,de->bte', seq, W_r)
        xh = jnp.einsum('btd,de->bte', seq, W)

        def step(h, xs):
            xzt, xrt, xht = xs
            z = jax.nn.sigmoid(xzt + h @ U_z + vz)
            r = jax.nn.sigmoid(xrt + h @ U_r + vr)
            hh = jnp.tanh(xht + r * h @ U + vh)
            h_new = (1.0 - z) * h + z * hh
            return (h_new, h_new)
        h0 = jnp.zeros((seq.shape[0], U.shape[0]), seq.dtype)
        xs = (jnp.swapaxes(xz, 0, 1), jnp.swapaxes(xr, 0, 1), jnp.swapaxes(xh, 0, 1))
        _, out_t = jax.lax.scan(step, h0, xs)
        return jnp.swapaxes(out_t, 0, 1)

    def _L0_ffn_ref(x, gate, W1, b1, W2, b2):
        import jax, jax.numpy as jnp
        import numpy as np
        B, T, D, H, E = (4, 256, 128, 256, 8)
        TOP_K = int(E * 0.25)
        raw_gate = jax.nn.softmax(jnp.einsum('btd,de->bte', x, gate), axis=-1)
        topk_scores, topk_idx = jax.lax.top_k(raw_gate, TOP_K)
        mask = jax.nn.one_hot(topk_idx, E, dtype=raw_gate.dtype).sum(axis=-2)
        gate_topk = mask * raw_gate
        gate_topk = gate_topk / jnp.maximum(gate_topk.sum(axis=-1, keepdims=True), 1e-12)
        h = jax.nn.relu(jnp.einsum('btd,edh->beth', x, W1) + b1[None, :, None, :])
        expert_out = jnp.einsum('beth,ehd->betd', h, W2) + b2[None, :, None, :]
        out = jnp.einsum('bte,betd->btd', gate_topk, expert_out)
        return out
    x = x + _L0_attn_ref(_L0_cond_ref(x, cond_1024, L0_cond_Wx, L0_cond_Wh, L0_cond_b), L0_attn_W_qkv, L0_attn_b_qkv, L0_attn_ln_w, L0_attn_ln_b)
    x = x + _L0_ffn_ref(_L0_cond2_ref(cond_1024, x, L0_cond2_W_z, L0_cond2_U_z, L0_cond2_C_z, L0_cond2_b_z, L0_cond2_W_r, L0_cond2_U_r, L0_cond2_C_r, L0_cond2_b_r, L0_cond2_W, L0_cond2_U, L0_cond2_C, L0_cond2_b), L0_ffn_gate, L0_ffn_W1, L0_ffn_b1, L0_ffn_W2, L0_ffn_b2)
    return x

_drawn_inputs = setup_inputs


def setup_inputs(seed=0):
    import zlib

    import numpy as np

    out = dict(_drawn_inputs(seed))
    spreads = {'L0_cond_b': (0.0, 0.1),
     'L0_attn_ln_w': (1.0, 0.2),
     'L0_attn_ln_b': (0.0, 0.1),
     'L0_cond2_b_z': (0.0, 2.0),
     'L0_cond2_b_r': (0.0, 2.0),
     'L0_cond2_b': (0.0, 0.1),
     'L0_ffn_b1': (0.0, 0.1),
     'L0_ffn_b2': (0.0, 0.1)}
    factors = {'L0_cond2_W_z': 6.875,
     'L0_cond2_U_z': 41.514,
     'L0_cond2_C_z': 8.0,
     'L0_cond2_W_r': 23.92,
     'L0_cond2_U_r': 200.0,
     'L0_cond2_C_r': 22.896,
     'L0_cond2_U': 5.36}
    for name, (base, spread) in spreads.items():
        noise = np.random.default_rng([zlib.crc32(name.encode()), seed]).standard_normal(out[name].shape)
        drawn = base * np.exp(spread * noise) if base else spread * noise
        out[name] = jnp.asarray(drawn.astype(out[name].dtype))
    for name, factor in factors.items():
        out[name] = (out[name] * factor).astype(out[name].dtype)
    return out
```

```python
from contextlib import ExitStack

import concourse.bass as bass
from concourse import mybir

F32 = mybir.dt.float32
BF16 = mybir.dt.bfloat16
FP16 = mybir.dt.float16
ALU = mybir.AluOpType
ACT = mybir.ActivationFunctionType
AX = mybir.AxisListType

D = 128
SPAN = 32
LN_EPS = 1e-5
NE, HID = 8, 256
HSCALE = 4096.0
PARTS_W, PARTS_H = 3, 2
PROD_FIRST = [(2, 0), (1, 0), (0, 0)]
PROD_SECOND = [(1, 1), (0, 1)]
PROD_X = [(2, 0), (1, 1), (0, 2), (1, 0), (0, 1), (0, 0)]


def adaln_kernel(nc: bass.Bass, t_in, out: bass.AP):
    B, T, _ = t_in["x"].shape
    C = SPAN
    NCH = T // C
    R = C * B
    TOK = T * B
    NT = TOK // 128
    KH = HID // 128
    HALF = 512

    LH = 0
    GH = LH + 4 * D
    QKV = GH + 3 * D
    NSTATE = QKV + 3 * D
    LX = NSTATE
    GX = LX + 4 * D
    NW = GX + 3 * D
    SCORE_SCALE = 1.0 / float(D * SPAN) ** 0.5

    with ExitStack() as ctx:
        def sb(name, shape, dt=F32):
            return ctx.enter_context(nc.sbuf_tensor(name, shape, dt))

        def pb(name, shape=(128, 512)):
            return ctx.enter_context(nc.psum_tensor(name, list(shape), F32))

        def sem(name):
            return ctx.enter_context(nc.semaphore(name))

        wall = sb("wall", [128, NW])
        wrest = sb("wrest", [128, NW])
        wparts = sb("wparts", [128, PARTS_W, NW], BF16)
        cw = sb("cw", [128, 3 * D])
        condT = sb("condT", [128, B])
        xrows = sb("xrows", [R, NCH, D])
        xrest = sb("xrest", [128, TOK])
        xTparts = sb("xTparts", [128, 3, TOK], BF16)
        xchunk = sb("xchunk", [128, 3, R], BF16)
        ident = sb("ident", [128, 128])
        lnw = sb("lnw", [R, D])
        lnb = sb("lnb", [R, D])
        bqk = sb("bqk", [128, 2])
        bv = sb("bv", [2 * R, D])
        bias_in = sb("bias_in", [B, 7 * D])
        bias_sum = sb("bias_sum", [B, 7 * D])
        bias_rest = sb("bias_rest", [B, 7 * D])
        bias_p = sb("bias_p", [B, 7 * D], BF16)
        bias_rows = sb("bias_rows", [128, 7 * D], BF16)
        onehot = sb("onehot", [128, C, B], BF16)
        batch_rows = sb("batch_rows", [B, C * 2, B])
        mask = sb("mask", [128, R])
        neghalf = sb("neghalf", [R, 1])

        lstm_h = [sb(f"lstm_h{p}", [128, C + 1, B], FP16) for p in range(PARTS_H)]
        lstm_hf = sb("lstm_hf", [128, 2, B])
        l_gates = sb("l_gates", [128, 6 * B])
        l_g = sb("l_g", [128, 2 * B])
        l_c = sb("l_c", [128, 2 * B])
        l_tc = sb("l_tc", [128, B])

        gru_h1 = sb("gru_h1", [128, C + 1, 3 * B], FP16)
        gru_hf = sb("gru_hf", [128, C + 1, 3 * B])
        gru_h2 = sb("gru_h2", [128, C + 1, B], FP16)
        g_mul = sb("g_mul", [128, 3 * B])
        g_add = sb("g_add", [128, 3 * B])
        g_r = sb("g_r", [128, B])
        g_zc = sb("g_zc", [128, B])
        g_rh = [sb(f"g_rh{p}", [128, B], FP16) for p in range(PARTS_H)]
        g_rhf = sb("g_rhf", [128, B])

        qT = sb("qT", [128, R])
        kT = sb("kT", [128, 2 * R])
        vrows = sb("vrows", [2 * R, D])
        sT = sb("sT", [2 * R, R])
        stats = sb("stats", [R, 6])
        aggr = sb("aggr", [R, 2])
        var_eps = sb("var_eps", [R, 1])
        rstd = sb("rstd", [R, 1])
        centred = sb("centred", [R, D])
        xln = sb("xln", [R, D])
        x2rows = sb("x2rows", [R, D])
        x2parts = [sb(f"x2parts{p}", [128, R], BF16) for p in range(3)]
        x2rest = sb("x2rest", [128, R])
        hT = sb("hT", [128, TOK])

        gate_w = sb("gate_w", [128, NE])
        w1 = sb("w1", [128, NE, HID])
        w2 = sb("w2", [128, NE, KH, D])
        b1 = sb("b1", [128, NE, KH])
        b2 = sb("b2", [NE, D])
        logits = sb("logits", [128, NT, NE])
        top = sb("top", [128, NT, 8])
        raw_gate = sb("raw_gate", [128, NT, NE])
        struck = sb("struck", [128, NT, NE])
        gates = sb("gates", [128, NT, NE])
        row_a = sb("row_a", [128, NT])
        row_b = sb("row_b", [128, NT])
        gates_T = sb("gates_T", [NE, TOK])
        hidden = sb("hidden", [128, 2, KH, TOK])
        acc = sb("acc", [128, NT, D])

        x2_dram = nc.dram_tensor("x2_scratch", [TOK, D], F32, kind="Internal").ap()

        p_lstm = pb("p_lstm")
        p_r = pb("p_r")
        p_zc = pb("p_zc")
        p_qk = pb("p_qk")
        p_v = pb("p_v")
        p_s = pb("p_s")
        p_o = pb("p_o")
        p_t = pb("p_t")
        lstm_pre = p_lstm[:, 0:C * 4 * B].rearrange("p (t g b) -> p t g b", g=4, b=B)
        r_pre = p_r[:, 0:R].rearrange("p (t b) -> p t b", b=B)
        zc_pre = p_zc[:, 0:2 * R].rearrange("p (t g b) -> p t g b", g=2, b=B)

        xT_bank = [p_qk, p_v]
        hid_bank = [p_lstm, p_r, p_zc, p_t]
        eo_bank = [p_s, p_o]
        gT_bank = [p_qk, p_v]

        lstm_w_in = sem("lstm_w_in")
        rest_w_in = sem("rest_w_in")
        cond_in = sem("cond_in")
        small_in = sem("small_in")
        SMALL = 8
        x_in = sem("x_in")
        ffn_in = sem("ffn_in")
        x2_saved = sem("x2_saved")
        x2_back = sem("x2_back")
        stored = sem("stored")
        pool_step = sem("pool_step")
        dve_step = sem("dve_step")
        ident_ready = sem("ident_ready")
        batch_rows_ready = sem("batch_rows_ready")
        consts_ready = sem("consts_ready")
        same_pre = sem("same_pre")
        mask_same = sem("mask_same")
        mask_ready = sem("mask_ready")
        xT_pre = sem("xT_pre")
        xT_ready = sem("xT_ready")
        vz_pre = sem("vz_pre")
        first_pre = sem("first_pre")
        bias_ready = sem("bias_ready")
        lstm_w_ready = sem("lstm_w_ready")
        rest_w_ready = sem("rest_w_ready")
        chunk_sems = []

        def csem(name):
            chunk_sems.append(sem(name))
            return chunk_sems[-1]

        lstm_h1_ready = csem("lstm_h1_ready")
        lstm_hf_ready = csem("lstm_hf_ready")
        lstm_h2_ready = csem("lstm_h2_ready")
        lstm_pre_ready = csem("lstm_pre_ready")
        lstm_sig_ready = csem("lstm_sig_ready")
        lstm_g_ready = csem("lstm_g_ready")
        lstm_fc_ready = csem("lstm_fc_ready")
        lstm_c_ready = csem("lstm_c_ready")
        lstm_tc_ready = csem("lstm_tc_ready")
        gru_h1_ready = csem("gru_h1_ready")
        gru_hf_ready = csem("gru_hf_ready")
        gru_h2_ready = csem("gru_h2_ready")
        gru_r_pre_ready = csem("gru_r_pre_ready")
        gru_z_pre_ready = csem("gru_z_pre_ready")
        gru_c_pre_ready = csem("gru_c_pre_ready")
        gru_r_ready = csem("gru_r_ready")
        gru_z_ready = csem("gru_z_ready")
        gru_zc_ready = csem("gru_zc_ready")
        gru_u_ready = csem("gru_u_ready")
        gru_rh1_ready = csem("gru_rh1_ready")
        gru_rhf_ready = csem("gru_rhf_ready")
        gru_rh2_ready = csem("gru_rh2_ready")
        gru_t_ready = csem("gru_t_ready")
        xchunk_ready = csem("xchunk_ready")
        xln_ready = csem("xln_ready")
        q_pre_ready = csem("q_pre_ready")
        k_pre_ready = csem("k_pre_ready")
        v_pre_ready = csem("v_pre_ready")
        q_ready = csem("q_ready")
        k_ready = csem("k_ready")
        v_ready = csem("v_ready")
        s_pre_ready = csem("s_pre_ready")
        s_ready = csem("s_ready")
        o_ready = csem("o_ready")
        ln_step = csem("ln_step")
        var_ready = csem("var_ready")
        rstd_ready = csem("rstd_ready")
        x2_ready = csem("x2_ready")
        x2T_ready = csem("x2T_ready")
        x2_split = csem("x2_split")
        x2p_ready = csem("x2p_ready")
        chunk_done = sem("chunk_done")
        chunk_clearing = sem("chunk_clearing")
        chunk_entered = sem("chunk_entered")
        chunk_go = sem("chunk_go")
        logits_pre = sem("logits_pre")
        f_dve = sem("f_dve")
        exp_ready = sem("exp_ready")
        gates_ready = sem("gates_ready")
        gT_pre = sem("gT_pre")
        gT_ready = sem("gT_ready")
        acc0_pre = sem("acc0_pre")
        hid_pre = sem("hid_pre")
        hid_ready = sem("hid_ready")
        eo_pre = sem("eo_pre")
        acc_ready = sem("acc_ready")

        block = ctx.enter_context(nc.Block())

        def w(part, col):
            return wparts[:, part, col:col + D]

        def phase_end(eng, n):
            eng.drain().then_inc(chunk_done, 1)
            eng.wait_ge(chunk_go, n + 1)
            eng.sem_inc(chunk_entered, 1)


        @block.sync
        def _(sp):
            def load(dst, src, s):
                sp.dma_start(dst, src).then_inc(s, 16)

            load(wall[:, LX:LX + 4 * D], t_in["L0_cond_Wx"], lstm_w_in)
            load(wall[:, LH:LH + 4 * D], t_in["L0_cond_Wh"], lstm_w_in)
            load(wall[:, QKV:QKV + 3 * D], t_in["L0_attn_W_qkv"], rest_w_in)
            for g, n in enumerate(("L0_cond2_U_r", "L0_cond2_U_z", "L0_cond2_U")):
                load(wall[:, GH + g * D:GH + (g + 1) * D], t_in[n], rest_w_in)
            for g, n in enumerate(("L0_cond2_W_r", "L0_cond2_W_z", "L0_cond2_W")):
                load(wall[:, GX + g * D:GX + (g + 1) * D], t_in[n], rest_w_in)
            load(gate_w[:, :], t_in["L0_ffn_gate"], ffn_in)
            load(w1[:, :, :], t_in["L0_ffn_W1"].rearrange("e d h -> d e h"), ffn_in)
            load(w2[:, :, :, :], t_in["L0_ffn_W2"].rearrange("e (k p) d -> p e k d", p=128), ffn_in)
            sp.dma_start(b1[:, :, :], t_in["L0_ffn_b1"].rearrange("e (k p) -> p e k", p=128),
                         allow_slow_non_contiguous=True).then_inc(ffn_in, 16)
            load(b2[:, :], t_in["L0_ffn_b2"], ffn_in)

            def end_phase(n):
                sp.wait_ge(chunk_done, 4 * (n + 1))
                sp.sem_inc(chunk_clearing, 1)
                for s in chunk_sems:
                    sp.sem_clear(s)
                sp.drain().then_inc(chunk_go, 1)

            def save_x2(n):
                sp.wait_ge(x2_ready, 1)
                sp.dma_start(x2_dram[bass.ds(n * R, R), :], x2rows[:, :]).then_inc(x2_saved, 16)

            save_x2(0)
            end_phase(0)
            with sp.Fori(1, NCH) as n:
                save_x2(n)
                end_phase(n)
            sp.wait_ge(x2_saved, 16 * NCH)
            sp.dma_start(acc[:, :, :], x2_dram.rearrange("(k p) d -> p k d", p=128)).then_inc(x2_back, 16)
            end_phase(NCH)
            steps = 128 // B
            for k in range(NT):
                sp.wait_ge(acc_ready, NE * NT + k + 1)
                for b in range(B):
                    sp.dma_start(out[b, k * steps:(k + 1) * steps, :], acc[b:128:B, k, :]).then_inc(stored, 16)
            sp.wait_ge(stored, 16 * NT * B)

        @block.gpsimd
        def _(pool):
            pool.memset(ident[:, :], 0.0).then_inc(pool_step, 1)
            pool.memset(batch_rows[:, :, :], 0.0).then_inc(pool_step, 1)
            pool.memset(onehot[:, :, :], 0.0).then_inc(pool_step, 1)
            pool.wait_ge(pool_step, 3)
            pool.affine_select(out=ident[:, :], in_=ident[:, :], compare_op=ALU.not_equal, fill=1.0, base=0,
                               pattern=[[-1, 128]], channel_multiplier=1).then_inc(ident_ready, 1)
            pool.affine_select(out=batch_rows[:, :, :], in_=batch_rows[:, :, :], compare_op=ALU.not_equal, fill=1.0,
                               base=0, pattern=[[0, 2 * C], [-1, B]], channel_multiplier=1).then_inc(batch_rows_ready, 1)
            for q in range(3):
                pool.affine_select(out=onehot[:, :, :], in_=onehot[:, :, :], compare_op=ALU.not_equal, fill=1.0,
                                   base=-32 * q, pattern=[[0, C], [-1, B]], channel_multiplier=1).then_inc(pool_step, 1)
                pool.wait_ge(pool_step, 4 + q)
            pool.memset(kT[:, 0:R], 0.0)
            pool.memset(vrows[0:R, :], 0.0)
            pool.memset(neghalf[:, :], -0.5)
            for p in range(PARTS_H):
                pool.memset(lstm_h[p][:, 0, :], 0.0)
            pool.memset(gru_h1[:, 0, :], 0.0)
            pool.memset(gru_hf[:, 0, :], 0.0)
            pool.memset(gru_h2[:, 0, :], 0.0)
            pool.memset(l_c[:, :], 0.0)
            pool.memset(l_g[:, :], 0.0)
            pool.memset(g_mul[:, :], 0.0)
            pool.memset(g_add[:, :], 0.0).then_inc(pool_step, 1)
            pool.wait_ge(pool_step, 7)
            pool.memset(g_add[:, 0:3 * B:3], HSCALE).then_inc(consts_ready, 1)
            pool.wait_ge(consts_ready, 1)
            pool.wait_ge(mask_same, 1)
            pool.affine_select(out=mask[0:R, :], in_=mask[0:R, :], compare_op=ALU.is_gt, fill=0.0, base=0,
                               pattern=[[-1, R]], channel_multiplier=1).then_inc(mask_ready, 1)
            pool.affine_select(out=mask[R:2 * R, :], in_=mask[R:2 * R, :], compare_op=ALU.is_ge, fill=0.0, base=0,
                               pattern=[[1, R]], channel_multiplier=-1).then_inc(mask_ready, 1)

            def phase(n, lstm, gru, more):
                if lstm:
                    pool.tensor_tensor(xln[:, :], xrows[:, bass.ds(n, 1), :].rearrange("r n d -> r (n d)"), lnb[:, :],
                                       ALU.add).then_inc(xln_ready, 1)
                    pool.wait_ge(xln_ready, 1)
                if more:
                    pool.tensor_copy(xchunk[:, :, :], xTparts[:, :, bass.ds((n + 1) * R, R)]).then_inc(xchunk_ready, 1)
                if gru:
                    pool.wait_ge(gru_h2_ready, C)
                    pool.tensor_copy(hT[:, bass.ds((n - 1) * R, R)].rearrange("p (t b) -> p t b", b=B),
                                     gru_hf[:, 1:, 2:3 * B:3])
                    pool.tensor_copy(gru_hf[:, 0, :], gru_hf[:, C, :])
                    pool.tensor_copy(gru_h1[:, 0, :], gru_h1[:, C, :])
                    pool.tensor_copy(gru_h2[:, 0, :], gru_h2[:, C, :])
                if lstm:
                    pool.wait_ge(lstm_h2_ready, C)
                    for p in range(PARTS_H):
                        pool.tensor_copy(lstm_h[p][:, 0, :], lstm_h[p][:, C, :])
                    pool.wait_ge(var_ready, 1)
                    pool.tensor_tensor(rstd[:, :], var_eps[:, :], neghalf[:, :], ALU.pow).then_inc(rstd_ready, 1)
                    pool.wait_ge(rstd_ready, 1)
                phase_end(pool, n)

            pool.wait_ge(x_in, 16 * B)
            pool.wait_ge(small_in, 16 * SMALL)
            pool.wait_ge(xT_ready, 1)
            pool.wait_ge(mask_ready, 2)
            pool.wait_ge(first_pre, 1)
            phase(0, True, False, True)
            with pool.Fori(1, NCH - 1) as n:
                phase(n, True, True, True)
            phase(NCH - 1, True, True, False)
            phase(NCH, False, True, False)

        @block.scalar
        def _(act):
            for b in range(B):
                act.dma_start(xrows[b:R:B, :, :], t_in["x"][b].rearrange("(n t) d -> t n d", t=C)).then_inc(x_in, 16)
            act.dma_start(condT[:, :], t_in["cond_1024"].rearrange("b d -> d b"),
                          allow_slow_non_contiguous=True).then_inc(cond_in, 16)
            for g, n in enumerate(("L0_cond2_C_r", "L0_cond2_C_z", "L0_cond2_C")):
                act.dma_start(cw[:, g * D:(g + 1) * D], t_in[n]).then_inc(cond_in, 16)
            n_small = 0

            def small(dst, src):
                act.dma_start(dst, src).then_inc(small_in, 16)
                return 1

            n_small += small(bias_in[:, 0:4 * D], t_in["L0_cond_b"].partition_broadcast(B))
            for g, n in enumerate(("L0_cond2_b_r", "L0_cond2_b_z", "L0_cond2_b")):
                n_small += small(bias_in[:, (4 + g) * D:(5 + g) * D], t_in[n].partition_broadcast(B))
            n_small += small(lnw[:, :], t_in["L0_attn_ln_w"].partition_broadcast(R))
            n_small += small(lnb[:, :], t_in["L0_attn_ln_b"].partition_broadcast(R))
            act.dma_start(bqk[:, :], t_in["L0_attn_b_qkv"][0:2 * D].rearrange("(k p) -> p k", p=128),
                          allow_slow_non_contiguous=True).then_inc(small_in, 16)
            n_small += 1
            n_small += small(bv[R:2 * R, :], t_in["L0_attn_b_qkv"][2 * D:3 * D].partition_broadcast(R))
            assert n_small == SMALL

            def phase(n, lstm, gru):
                for s in range(C):
                    if gru:
                        act.wait_ge(gru_r_pre_ready, s + 1)
                        act.activation(g_r[:, :], r_pre[:, s, :], ACT.Sigmoid).then_inc(gru_r_ready, 1)
                        act.wait_ge(gru_z_pre_ready, s + 1)
                        act.activation(g_mul[:, 1:3 * B:3], zc_pre[:, s, 0, :], ACT.Sigmoid).then_inc(gru_z_ready, 1)
                        act.activation(g_zc[:, :], zc_pre[:, s, 0, :], ACT.Sigmoid, scale=-1.0).then_inc(gru_zc_ready, 1)
                    if lstm:
                        act.wait_ge(lstm_pre_ready, s + 1)
                        act.activation(l_gates[:, 0:6 * B:2], p_lstm[:, 4 * B * s:4 * B * s + 3 * B],
                                       ACT.Sigmoid).then_inc(lstm_sig_ready, 1)
                        act.activation(l_g[:, 1:2 * B:2], p_lstm[:, 4 * B * s + 3 * B:4 * B * (s + 1)],
                                       ACT.Tanh).then_inc(lstm_g_ready, 1)
                    if gru:
                        act.wait_ge(gru_c_pre_ready, s + 1)
                        act.activation(g_mul[:, 2:3 * B:3], zc_pre[:, s, 1, :], ACT.Tanh).then_inc(gru_t_ready, 1)
                    if lstm:
                        act.wait_ge(lstm_c_ready, s + 1)
                        act.activation(l_tc[:, :], l_c[:, 1:2 * B:2], ACT.Tanh).then_inc(lstm_tc_ready, 1)
                if lstm:
                    act.wait_ge(q_pre_ready, 1)
                    act.activation(qT[:, :], p_qk[:, 0:R], ACT.Identity, bias=bqk[:, 0:1]).then_inc(q_ready, 1)
                    act.wait_ge(s_pre_ready, 1)
                    act.activation(kT[:, 0:R], kT[:, R:2 * R], ACT.Copy)
                    act.wait_ge(o_ready, 1)
                    act.activation(vrows[0:R, :], vrows[R:2 * R, :], ACT.Copy)
                phase_end(act, n)

            act.wait_ge(consts_ready, 1)
            act.wait_ge(small_in, 16 * SMALL)
            phase(0, True, False)
            with act.Fori(1, NCH) as n:
                phase(n, True, True)
            phase(NCH, False, True)

            act.wait_ge(ffn_in, 16 * 5)
            act.wait_ge(f_dve, 3)
            act.activation(logits[:, :, :], logits[:, :, :], ACT.Exp, scale=1.0 / HSCALE).then_inc(exp_ready, 1)
            i = 0
            for e in range(NE):
                for k in range(KH):
                    for h in range(TOK // HALF):
                        act.wait_ge(hid_pre, i + 1)
                        if e >= 2:
                            act.wait_ge(eo_pre, (e - 1) * NT)
                        act.activation(hidden[:, e % 2, k, h * HALF:(h + 1) * HALF], hid_bank[i % 4][:, :], ACT.Relu,
                                       bias=b1[:, e, k:k + 1], scale=1.0 / HSCALE).then_inc(hid_ready, 1)
                        i += 1

        @block.vector
        def _(dve):
            def link(ins, n=[0]):
                n[0] += 1
                ins.then_inc(dve_step, 1)
                dve.wait_ge(dve_step, n[0])

            def split3(parts, src, rest, scale=None):
                if scale is None:
                    link(dve.tensor_copy(parts[0], src))
                    link(dve.tensor_tensor(rest, src, parts[0], ALU.subtract))
                else:
                    link(dve.tensor_scalar(parts[0], src, scale, None, ALU.mult))
                    link(dve.scalar_tensor_tensor(out=rest, in0=src, scalar=scale, in1=parts[0],
                                                  op0=ALU.mult, op1=ALU.subtract))
                link(dve.tensor_copy(parts[1], rest))
                return dve.tensor_tensor(parts[2], rest, parts[1], ALU.subtract)

            def split_w(lo, hi, scale=None):
                return split3([wparts[:, p, lo:hi] for p in range(3)], wall[:, lo:hi], wrest[:, lo:hi], scale)

            link(dve.memset(bias_rows[:, :], 0.0))
            link(dve.memset(top[:, :, :], -1.0))
            dve.wait_ge(lstm_w_in, 32)
            split_w(LX, LX + 4 * D).then_inc(lstm_w_ready, 1)
            for h in range(TOK // HALF):
                dve.wait_ge(xT_pre, (h + 1) * (HALF // R))
                ins = split3([xTparts[:, p, h * HALF:(h + 1) * HALF] for p in range(3)], xT_bank[h][:, :],
                             xrest[:, h * HALF:(h + 1) * HALF])
                link(ins)
            link(dve.tensor_copy(xchunk[:, :, :], xTparts[:, :, 0:R]))
            dve.sem_inc(xT_ready, 1)
            split_w(LH, LH + 4 * D, 1.0 / HSCALE).then_inc(lstm_w_ready, 1)
            dve.wait_ge(small_in, 16 * SMALL)
            dve.wait_ge(vz_pre, 1)
            link(dve.tensor_copy(bias_sum[:, 0:4 * D], bias_in[:, 0:4 * D]))
            link(dve.tensor_tensor(bias_sum[:, 4 * D:7 * D], p_s[0:B, 0:3 * D], bias_in[:, 4 * D:7 * D], ALU.add))
            link(dve.tensor_copy(bias_p[:, :], bias_sum[:, :]))
            link(dve.tensor_copy(bias_rows[0:B, :], bias_p[:, :]))
            link(dve.tensor_tensor(bias_rest[:, :], bias_sum[:, :], bias_p[:, :], ALU.subtract))
            link(dve.tensor_copy(bias_p[:, :], bias_rest[:, :]))
            link(dve.tensor_copy(bias_rows[32:32 + B, :], bias_p[:, :]))
            dve.tensor_tensor(bias_rows[64:64 + B, :], bias_rest[:, :], bias_p[:, :], ALU.subtract).then_inc(bias_ready, 1)
            dve.wait_ge(same_pre, 1)
            dve.tensor_scalar(mask[:, :], p_o[:, 0:R], SCORE_SCALE, None, ALU.mult).then_inc(mask_same, 1)
            dve.wait_ge(rest_w_in, 16 * 7)
            link(split_w(GH, NSTATE, 1.0 / HSCALE))
            split_w(GX, NW).then_inc(rest_w_ready, 1)
            dve.wait_ge(consts_ready, 1)
            dve.wait_ge(mask_ready, 2)

            def h_of(t, s):
                return t[:, s, 2:3 * B:3]

            def gru_update(s):
                dve.wait_ge(gru_zc_ready, s + 1)
                if s:
                    dve.wait_ge(gru_hf_ready, s)
                dve.tensor_tensor(g_add[:, 2:3 * B:3], g_zc[:, :], h_of(gru_hf, s), ALU.mult).then_inc(gru_u_ready, 1)

            def gru_reset(s):
                dve.wait_ge(gru_r_ready, s + 1)
                if s:
                    dve.wait_ge(gru_hf_ready, s)
                dve.tensor_tensor(g_rh[0][:, :], g_r[:, :], h_of(gru_hf, s), ALU.mult).then_inc(gru_rh1_ready, 1)
                dve.tensor_tensor(g_rhf[:, :], g_r[:, :], h_of(gru_hf, s), ALU.mult).then_inc(gru_rhf_ready, 1)
                dve.wait_ge(gru_rhf_ready, s + 1)
                dve.tensor_tensor(g_rh[1][:, :], g_rhf[:, :], g_rh[0][:, :], ALU.subtract).then_inc(gru_rh2_ready, 1)

            def gru_state(s):
                dve.wait_ge(gru_t_ready, s + 1)
                dve.wait_ge(gru_u_ready, s + 1)
                dve.tensor_tensor_scan(gru_h1[:, s + 1, :], g_mul[:, :], g_add[:, :], 0.0,
                                       ALU.mult, ALU.add).then_inc(gru_h1_ready, 1)
                dve.tensor_tensor_scan(gru_hf[:, s + 1, :], g_mul[:, :], g_add[:, :], 0.0,
                                       ALU.mult, ALU.add).then_inc(gru_hf_ready, 1)
                dve.wait_ge(gru_hf_ready, s + 1)
                dve.tensor_tensor(gru_h2[:, s + 1, :], h_of(gru_hf, s + 1), h_of(gru_h1, s + 1),
                                  ALU.subtract).then_inc(gru_h2_ready, 1)

            def lstm_cell(s):
                dve.wait_ge(lstm_sig_ready, s + 1)
                if s:
                    dve.wait_ge(lstm_c_ready, s)
                dve.tensor_tensor(l_gates[:, 1:2 * B:2], l_gates[:, 2 * B:4 * B:2], l_c[:, 1:2 * B:2],
                                  ALU.mult).then_inc(lstm_fc_ready, 1)
                dve.wait_ge(lstm_g_ready, s + 1)
                dve.wait_ge(lstm_fc_ready, s + 1)
                dve.tensor_tensor_scan(l_c[:, :], l_g[:, :], l_gates[:, 0:2 * B], 0.0,
                                       ALU.mult, ALU.add).then_inc(lstm_c_ready, 1)

            def lstm_state(s):
                o = l_gates[:, 4 * B:6 * B:2]
                dve.wait_ge(lstm_tc_ready, s + 1)
                dve.scalar_tensor_tensor(out=lstm_h[0][:, s + 1, :], in0=o, scalar=HSCALE, in1=l_tc[:, :],
                                         op0=ALU.mult, op1=ALU.mult).then_inc(lstm_h1_ready, 1)
                dve.scalar_tensor_tensor(out=lstm_hf[:, s % 2, :], in0=o, scalar=HSCALE, in1=l_tc[:, :],
                                         op0=ALU.mult, op1=ALU.mult).then_inc(lstm_hf_ready, 1)
                dve.wait_ge(lstm_hf_ready, s + 1)
                dve.tensor_tensor(lstm_h[1][:, s + 1, :], lstm_hf[:, s % 2, :], lstm_h[0][:, s + 1, :],
                                  ALU.subtract).then_inc(lstm_h2_ready, 1)

            def attention(n, saved):
                dve.wait_ge(k_pre_ready, 1)
                dve.tensor_scalar(kT[:, R:2 * R], p_o[:, 0:R], bqk[:, 1:2], None, ALU.add).then_inc(k_ready, 1)
                dve.wait_ge(v_pre_ready, 1)
                dve.tensor_tensor(vrows[R:2 * R, :], p_v[R:2 * R, 0:D], bv[R:2 * R, :], ALU.add).then_inc(v_ready, 1)
                dve.wait_ge(s_pre_ready, 1)
                dve.tensor_tensor(sT[:, :], p_s[:, 0:R], mask[:, :], ALU.mult).then_inc(s_ready, 1)
                dve.wait_ge(o_ready, 1)
                dve.bn_stats(stats[:, :], p_o[0:R, 0:D]).then_inc(ln_step, 1)
                dve.wait_ge(ln_step, 1)
                dve.bn_aggr(aggr[:, :], stats[:, :]).then_inc(ln_step, 1)
                dve.wait_ge(ln_step, 2)
                dve.tensor_scalar(var_eps[:, :], aggr[:, 1:2], LN_EPS, None, ALU.add).then_inc(var_ready, 1)
                dve.scalar_tensor_tensor(out=centred[:, :], in0=p_o[0:R, 0:D], scalar=aggr[:, 0:1], in1=lnw[:, :],
                                         op0=ALU.subtract, op1=ALU.mult).then_inc(ln_step, 1)
                dve.wait_ge(ln_step, 3)
                dve.wait_ge(rstd_ready, 1)
                dve.wait_ge(xln_ready, 1)
                if saved is not None:
                    dve.wait_ge(x2_saved, saved)
                dve.scalar_tensor_tensor(out=x2rows[:, :], in0=centred[:, :], scalar=rstd[:, 0:1], in1=xln[:, :],
                                         op0=ALU.mult, op1=ALU.add).then_inc(x2_ready, 1)
                dve.wait_ge(x2T_ready, 1)
                dve.tensor_copy(x2parts[0][:, :], p_t[:, 0:R]).then_inc(x2p_ready, 1)
                dve.wait_ge(x2p_ready, 1)
                dve.tensor_tensor(x2rest[:, :], p_t[:, 0:R], x2parts[0][:, :], ALU.subtract).then_inc(x2_split, 1)
                dve.wait_ge(x2_split, 1)
                dve.tensor_copy(x2parts[1][:, :], x2rest[:, :]).then_inc(x2p_ready, 1)
                dve.wait_ge(x2p_ready, 2)
                dve.tensor_tensor(x2parts[2][:, :], x2rest[:, :], x2parts[1][:, :], ALU.subtract).then_inc(x2p_ready, 1)

            def phase(n, lstm, gru, saved=None):
                for s in range(C):
                    if gru:
                        gru_reset(s)
                        gru_update(s)
                    if lstm:
                        lstm_cell(s)
                    if gru:
                        gru_state(s)
                    if lstm:
                        lstm_state(s)
                if lstm:
                    attention(n, saved)
                phase_end(dve, n)

            phase(0, True, False)
            with dve.Fori(1, NCH) as n:
                phase(n, True, True, 16 * n)
            phase(NCH, False, True)

            lg = p_qk[:, 0:NT * NE].rearrange("p (k e) -> p k e", e=NE)

            def over_experts(x):
                return x[:, :].unsqueeze(2).broadcast_to([128, NT, NE])

            def fstep(ins, n=[0]):
                n[0] += 1
                ins.then_inc(f_dve, 1)
                dve.wait_ge(f_dve, n[0])

            dve.wait_ge(logits_pre, 1)
            fstep(dve.tensor_copy(raw_gate[:, :, :], lg))
            fstep(dve.tensor_reduce(row_a[:, :], raw_gate[:, :, :], AX.X, ALU.max))
            fstep(dve.tensor_tensor(logits[:, :, :], raw_gate[:, :, :], over_experts(row_a), ALU.subtract))
            dve.wait_ge(exp_ready, 1)
            fstep(dve.tensor_reduce(row_a[:, :], logits[:, :, :], AX.X, ALU.add))
            fstep(dve.reciprocal(row_b[:, :], row_a[:, :]))
            fstep(dve.tensor_tensor(raw_gate[:, :, :], logits[:, :, :], over_experts(row_b), ALU.mult))
            for k in range(NT):
                ins = dve.max(logits[:, k, :], raw_gate[:, k, :])
            fstep(ins)
            fstep(dve.tensor_copy(top[:, :, 0:2], logits[:, :, 0:2]))
            for k in range(NT):
                ins = dve.match_replace(struck[:, k, :], top[:, k, :], raw_gate[:, k, :], -2.0)
            fstep(ins)
            fstep(dve.scalar_tensor_tensor(out=gates[:, :, :], in0=struck[:, :, :], scalar=0.0, in1=raw_gate[:, :, :],
                                           op0=ALU.is_lt, op1=ALU.mult))
            fstep(dve.tensor_reduce(row_a[:, :], gates[:, :, :], AX.X, ALU.add))
            fstep(dve.tensor_scalar(row_a[:, :], row_a[:, :], 1e-12, None, ALU.max))
            fstep(dve.reciprocal(row_b[:, :], row_a[:, :]))
            dve.tensor_tensor(gates[:, :, :], gates[:, :, :], over_experts(row_b), ALU.mult).then_inc(gates_ready, 1)
            for h in range(TOK // HALF):
                dve.wait_ge(gT_pre, h + 1)
                dve.tensor_copy(gates_T[:, h * HALF:(h + 1) * HALF], gT_bank[h][0:NE, :]).then_inc(gT_ready, 1)
            dve.wait_ge(x2_back, 16)
            for k in range(NT):
                dve.wait_ge(acc0_pre, k // 4 * 4 + 4)
                dve.tensor_tensor(acc[:, k, :], eo_bank[k // 4][:, k % 4 * D:(k % 4 + 1) * D], acc[:, k, :],
                                  ALU.add).then_inc(acc_ready, 1)
            dve.wait_ge(gates_ready, 1)
            for e in range(NE):
                for k in range(NT):
                    dve.wait_ge(eo_pre, e * NT + k // 4 * 4 + 4)
                    dve.wait_ge(acc_ready, e * NT + k + 1)
                    dve.scalar_tensor_tensor(out=acc[:, k, :], in0=eo_bank[k // 4][:, k % 4 * D:(k % 4 + 1) * D],
                                             scalar=gates[:, k, e:e + 1], in1=acc[:, k, :],
                                             op0=ALU.mult, op1=ALU.add).then_inc(acc_ready, 1)

        @block.tensor
        def _(pe):
            def mm(out_, lhsT, rhs, start=False):
                return pe.matmul(out_, lhsT, rhs, start=start, stop=True, skip_group_check=True)

            def lstm_from_x():
                for g in range(4):
                    mm(lstm_pre[:, :, g, :], bias_rows[:, g * D:(g + 1) * D], onehot[:, :, :], start=(g == 0))
                for g in range(4):
                    for a, b in PROD_X:
                        mm(lstm_pre[:, :, g, :], w(a, LX + g * D), xchunk[:, b, :].rearrange("p (t b) -> p t b", b=B))

            def gru_from_x():
                outs = [r_pre, zc_pre[:, :, 0, :], zc_pre[:, :, 1, :]]
                for g in range(3):
                    mm(outs[g], bias_rows[:, (4 + g) * D:(5 + g) * D], onehot[:, :, :], start=(g < 2))
                for i in range(3):
                    pe.wait_ge(x2p_ready, i + 1)
                    for g in range(3):
                        for a in range(3 - i):
                            mm(outs[g], w(a, GX + g * D), x2parts[i][:, :].rearrange("p (t b) -> p t b", b=B))

            pe.wait_ge(ident_ready, 1)
            pe.wait_ge(x_in, 16 * B)
            for n in range(NCH):
                h, j = n * R // HALF, n * R % HALF
                pe.transpose(xT_bank[h][:, j:j + R], xrows[:, n, :], ident[0:R, 0:R]).then_inc(xT_pre, 1)
            pe.wait_ge(cond_in, 16 * 4)
            mm(p_s[0:B, 0:3 * D], condT[:, :], cw[:, :], start=True).then_inc(vz_pre, 1)
            pe.wait_ge(batch_rows_ready, 1)
            keys = batch_rows[:, :, :].rearrange("p t b -> p (t b)")
            mm(p_o[:, 0:R], keys, keys[:, 0:R], start=True).then_inc(same_pre, 1)
            pe.wait_ge(bias_ready, 1)
            pe.wait_ge(consts_ready, 1)
            pe.wait_ge(lstm_w_ready, 2)
            pe.wait_ge(xT_ready, 1)
            lstm_from_x()
            for g in range(4):
                ins = mm(lstm_pre[:, 0, g, :], wall[:, LH + g * D:LH + (g + 1) * D], condT[:, :])
            ins.then_inc(first_pre, 1)

            def lstm_products(s, pairs):
                for g in range(4):
                    for a, b in pairs:
                        ins = mm(lstm_pre[:, s, g, :], w(a, LH + g * D), lstm_h[b][:, s, :])
                return ins

            def gru_products(out_, g, s, pairs):
                for a, b in pairs:
                    h = h_view[b](s)
                    ins = mm(out_, w(a, GH + g * D), h)
                return ins

            h_view = [lambda s: gru_h1[:, s, 2:3 * B:3], lambda s: gru_h2[:, s, :]]

            def phase(n, lstm, gru, more):
                for s in range(C):
                    if gru:
                        if s:
                            pe.wait_ge(gru_h1_ready, s)
                        gru_products(r_pre[:, s, :], 0, s, PROD_FIRST)
                        gru_products(zc_pre[:, s, 0, :], 1, s, PROD_FIRST)
                        if s:
                            pe.wait_ge(gru_h2_ready, s)
                        gru_products(r_pre[:, s, :], 0, s, PROD_SECOND).then_inc(gru_r_pre_ready, 1)
                        gru_products(zc_pre[:, s, 0, :], 1, s, PROD_SECOND).then_inc(gru_z_pre_ready, 1)
                    if lstm:
                        if s:
                            pe.wait_ge(lstm_h1_ready, s)
                        lstm_products(s, PROD_FIRST)
                        if s:
                            pe.wait_ge(lstm_h2_ready, s)
                        lstm_products(s, PROD_SECOND).then_inc(lstm_pre_ready, 1)
                    if gru:
                        pe.wait_ge(gru_zc_ready, s + 1)
                        pe.wait_ge(gru_rh1_ready, s + 1)
                        for a, b in PROD_FIRST:
                            mm(zc_pre[:, s, 1, :], w(a, GH + 2 * D), g_rh[b][:, :])
                        pe.wait_ge(gru_rh2_ready, s + 1)
                        for a, b in PROD_SECOND:
                            ins = mm(zc_pre[:, s, 1, :], w(a, GH + 2 * D), g_rh[b][:, :])
                        ins.then_inc(gru_c_pre_ready, 1)
                if lstm:
                    pe.wait_ge(lstm_h2_ready, C)
                    hp = [lstm_h[p][:, 1:, :].rearrange("p t b -> p (t b)") for p in range(PARTS_H)]
                    pairs = PROD_FIRST + PROD_SECOND
                    for i, (a, b) in enumerate(pairs):
                        ins = mm(p_qk[:, 0:R], w(a, QKV), hp[b], start=(i == 0))
                    ins.then_inc(q_pre_ready, 1)
                    for i, (a, b) in enumerate(pairs):
                        ins = mm(p_o[:, 0:R], w(a, QKV + D), hp[b], start=(i == 0))
                    ins.then_inc(k_pre_ready, 1)
                    for i, (a, b) in enumerate(pairs):
                        ins = mm(p_v[R:2 * R, 0:D], hp[b], w(a, QKV + 2 * D), start=(i == 0))
                    ins.then_inc(v_pre_ready, 1)
                    pe.wait_ge(q_ready, 1)
                    pe.wait_ge(k_ready, 1)
                    mm(p_s[:, 0:R], kT[:, :], qT[:, :], start=True).then_inc(s_pre_ready, 1)
                    pe.wait_ge(s_ready, 1)
                    pe.wait_ge(v_ready, 1)
                    mm(p_o[0:R, 0:D], sT[:, :], vrows[:, :], start=True).then_inc(o_ready, 1)
                    if more:
                        pe.wait_ge(xchunk_ready, 1)
                        lstm_from_x()
                    pe.wait_ge(x2_ready, 1)
                    pe.transpose(p_t[:, 0:R], x2rows[:, :], ident[0:R, 0:R]).then_inc(x2T_ready, 1)
                    if gru:
                        pe.wait_ge(gru_t_ready, C)
                    gru_from_x()
                phase_end(pe, n)

            pe.wait_ge(rest_w_ready, 1)
            phase(0, True, False, True)
            with pe.Fori(1, NCH - 1) as n:
                phase(n, True, True, True)
            phase(NCH - 1, True, True, False)
            phase(NCH, False, True, False)

            pe.wait_ge(ffn_in, 16 * 5)
            for k in range(NT):
                ins = mm(p_qk[:, k * NE:(k + 1) * NE], hT[:, k * 128:(k + 1) * 128], gate_w[:, :], start=(k == 0))
            ins.then_inc(logits_pre, 1)

            def hidden_rows(e):
                i = e * KH * (TOK // HALF)
                for k in range(KH):
                    for h in range(TOK // HALF):
                        if i >= 4:
                            pe.wait_ge(hid_ready, i - 3)
                        mm(hid_bank[i % 4][:, :], w1[:, e, k * 128:(k + 1) * 128], hT[:, h * HALF:(h + 1) * HALF],
                           start=True).then_inc(hid_pre, 1)
                        i += 1

            def expert_out(e):
                pe.wait_ge(hid_ready, (e + 1) * KH * (TOK // HALF))
                for k in range(NT):
                    if k % 4 == 0:
                        pe.wait_ge(acc_ready, e * NT + k + 4)
                    for j in range(KH):
                        ins = mm(eo_bank[k // 4][:, k % 4 * D:(k % 4 + 1) * D], hidden[:, e % 2, j, k * 128:(k + 1) * 128],
                                 w2[:, e, j, :], start=(k % 4 == 0 and j == 0))
                    ins.then_inc(eo_pre, 1)

            hidden_rows(0)
            pe.wait_ge(gates_ready, 1)
            for k in range(NT):
                h, j = divmod(k * 128, HALF)
                ins = pe.transpose(gT_bank[h][0:NE, j:j + 128], gates[:, k, :], ident[:, :])
                if k % 4 == 3:
                    ins.then_inc(gT_pre, 1)
            for k in range(NT):
                pe.wait_ge(gT_ready, k // 4 + 1)
                mm(eo_bank[k // 4][:, k % 4 * D:(k % 4 + 1) * D], gates_T[:, k * 128:(k + 1) * 128], b2[:, :],
                   start=(k % 4 == 0)).then_inc(acc0_pre, 1)
            for e in range(NE):
                if e + 1 < NE:
                    hidden_rows(e + 1)
                expert_out(e)


_INS = ["x", "cond_1024", "L0_cond_Wx", "L0_cond_Wh", "L0_cond_b", "L0_attn_W_qkv", "L0_attn_b_qkv",
        "L0_attn_ln_w", "L0_attn_ln_b", "L0_cond2_W_z", "L0_cond2_U_z", "L0_cond2_C_z", "L0_cond2_b_z",
        "L0_cond2_W_r", "L0_cond2_U_r", "L0_cond2_C_r", "L0_cond2_b_r", "L0_cond2_W", "L0_cond2_U",
        "L0_cond2_C", "L0_cond2_b", "L0_ffn_gate", "L0_ffn_W1", "L0_ffn_b1", "L0_ffn_W2", "L0_ffn_b2"]


def kernel(**inputs):
    import numpy as _np
    import concourse.bacc as _bacc
    from concourse import mybir as _mybir
    from concourse.bass_utils import run_bass_kernel_spmd as _run

    nc = _bacc.Bacc("TRN2", target_bir_lowering=False, num_devices=1)
    arrays, t_in = {}, {}
    for name in _INS:
        a = _np.ascontiguousarray(inputs[name])
        arrays[f"in_{name}"] = a
        t_in[name] = nc.dram_tensor(f"in_{name}", a.shape, _mybir.dt.from_np(a.dtype), kind="ExternalInput").ap()
    out = nc.dram_tensor("out_0", inputs["x"].shape, _mybir.dt.float32, kind="ExternalOutput").ap()
    adaln_kernel(nc, t_in, out)
    r = _run(nc, [arrays], core_ids=[0])
    return r.results[0]["out_0"]
```

```python
from contextlib import ExitStack

import concourse.bass as bass
from concourse import mybir

F32 = mybir.dt.float32
BF16 = mybir.dt.bfloat16
FP16 = mybir.dt.float16
ALU = mybir.AluOpType
ACT = mybir.ActivationFunctionType
AX = mybir.AxisListType

D = 128
SPAN = 32
LN_EPS = 1e-5
NE, HID = 8, 256
HSCALE = 4096.0
PARTS_W, PARTS_H = 3, 2
PROD_FIRST = [(2, 0), (1, 0), (0, 0)]
PROD_SECOND = [(1, 1), (0, 1)]
PROD_X = [(2, 0), (1, 1), (0, 2), (1, 0), (0, 1), (0, 0)]


def adaln_kernel(nc: bass.Bass, t_in, out: bass.AP):
    B, T, _ = t_in["x"].shape
    C = SPAN
    NCH = T // C
    SEG = 2 * C
    NSEG = T // SEG
    LAG = 12
    FIRST = C + LAG
    R = C * B
    TOK = T * B
    NT = TOK // 128
    KH = HID // 128
    HALF = 512

    LH = 0
    GH = LH + 4 * D
    QKV = GH + 3 * D
    NSTATE = QKV + 3 * D
    LX = NSTATE
    GX = LX + 4 * D
    NW = GX + 3 * D
    SCORE_SCALE = 1.0 / float(D * SPAN) ** 0.5

    with ExitStack() as ctx:
        def sb(name, shape, dt=F32):
            return ctx.enter_context(nc.sbuf_tensor(name, shape, dt))

        def pb(name, shape=(128, 512)):
            return ctx.enter_context(nc.psum_tensor(name, list(shape), F32))

        def sem(name):
            return ctx.enter_context(nc.semaphore(name))

        wall = sb("wall", [128, NW])
        wrest = sb("wrest", [128, NW])
        wparts = sb("wparts", [128, PARTS_W, NW], BF16)
        cw = sb("cw", [128, 3 * D])
        condT = sb("condT", [128, B])
        xrows = sb("xrows", [R, NCH, D])
        xrest = sb("xrest", [128, TOK])
        xTparts = sb("xTparts", [128, 3, TOK + R], BF16)
        xchunk = sb("xchunk", [128, 3, R], BF16)
        ident = sb("ident", [128, 128])
        lnw = sb("lnw", [R, D])
        lnb = sb("lnb", [R, D])
        bqk = sb("bqk", [128, 2])
        bv = sb("bv", [2 * R, D])
        bias_in = sb("bias_in", [B, 7 * D])
        bias_sum = sb("bias_sum", [B, 7 * D])
        bias_rest = sb("bias_rest", [B, 7 * D])
        bias_p = sb("bias_p", [B, 7 * D], BF16)
        bias_rows = sb("bias_rows", [128, 7 * D], BF16)
        onehot = sb("onehot", [128, C, B], BF16)
        batch_rows = sb("batch_rows", [B, C * 2, B])
        mask = sb("mask", [128, R])
        neghalf = sb("neghalf", [R, 1])

        lstm_h = [sb(f"lstm_h{p}", [128, SEG + 1, B], FP16) for p in range(PARTS_H)]
        lstm_hf = sb("lstm_hf", [128, 2, B])
        l_gates = sb("l_gates", [128, 6 * B])
        l_g = sb("l_g", [128, 2 * B])
        l_c = sb("l_c", [128, 2 * B])
        l_tc = sb("l_tc", [128, B])

        gru_h1 = sb("gru_h1", [128, SEG + 1, 3 * B], FP16)
        gru_hf = sb("gru_hf", [128, SEG + 1, 3 * B])
        gru_h2 = sb("gru_h2", [128, SEG + 1, B], FP16)
        g_mul = sb("g_mul", [128, 3 * B])
        g_add = sb("g_add", [128, 3 * B])
        g_r = sb("g_r", [128, B])
        g_zc = sb("g_zc", [128, B])
        g_rh = [sb(f"g_rh{p}", [128, B], FP16) for p in range(PARTS_H)]
        g_rhf = sb("g_rhf", [128, B])

        qT = sb("qT", [128, R])
        kT = sb("kT", [128, 2 * R])
        vrows = sb("vrows", [2 * R, D])
        sT = sb("sT", [2 * R, R])
        stats = sb("stats", [R, 6])
        aggr = sb("aggr", [R, 2])
        var_eps = sb("var_eps", [R, 1])
        rstd = sb("rstd", [R, 1])
        centred = sb("centred", [R, D])
        xln = sb("xln", [R, D])
        x2rows = sb("x2rows", [R, D])
        x2parts = [sb(f"x2parts{p}", [128, R], BF16) for p in range(3)]
        x2rest = sb("x2rest", [128, R])
        hist = sb("hist", [128, LAG * B + TOK])
        hT = hist[:, LAG * B:]

        gate_w = sb("gate_w", [128, NE])
        w1 = sb("w1", [128, NE, HID])
        w2 = sb("w2", [128, NE, KH, D])
        b1 = sb("b1", [128, NE, KH])
        b2 = sb("b2", [NE, D])
        logits = sb("logits", [128, NT, NE])
        top = sb("top", [128, NT, 8])
        raw_gate = sb("raw_gate", [128, NT, NE])
        struck = sb("struck", [128, NT, NE])
        gates = sb("gates", [128, NT, NE])
        row_a = sb("row_a", [128, NT])
        row_b = sb("row_b", [128, NT])
        gates_T = sb("gates_T", [NE, TOK])
        hidden = sb("hidden", [128, 2, KH, TOK])
        acc = sb("acc", [128, NT, D])

        x2_dram = nc.dram_tensor("x2_scratch", [TOK, D], F32, kind="Internal").ap()

        p_lstm = [pb(f"p_lstm{c}") for c in range(2)]
        p_r = [pb(f"p_r{c}") for c in range(2)]
        p_zc = [pb(f"p_zc{c}") for c in range(2)]
        p_a = pb("p_a")
        p_b = pb("p_b")
        lstm_pre = [p[:, 0:C * 4 * B].rearrange("p (t g b) -> p t g b", g=4, b=B) for p in p_lstm]
        r_pre = [p[:, 0:R].rearrange("p (t b) -> p t b", b=B) for p in p_r]
        zc_pre = [p[:, 0:2 * R].rearrange("p (t g b) -> p t g b", g=2, b=B) for p in p_zc]

        xT_bank = [p_a, p_b]
        p_vz, p_same = p_r[1], p_zc[1]
        hid_bank = p_lstm + p_r
        eo_bank = p_zc
        gT_bank = [p_a, p_b]

        lstm_w_in = sem("lstm_w_in")
        rest_w_in = sem("rest_w_in")
        cond_in = sem("cond_in")
        small_in = sem("small_in")
        SMALL = 8
        x_in = sem("x_in")
        ffn_in = sem("ffn_in")
        x2_saved = sem("x2_saved")
        x2_back = sem("x2_back")
        stored = sem("stored")
        pool_step = sem("pool_step")
        dve_step = sem("dve_step")
        ident_ready = sem("ident_ready")
        batch_rows_ready = sem("batch_rows_ready")
        consts_ready = sem("consts_ready")
        same_pre = sem("same_pre")
        mask_same = sem("mask_same")
        mask_ready = sem("mask_ready")
        xT_pre = sem("xT_pre")
        xT_ready = sem("xT_ready")
        vz_pre = sem("vz_pre")
        first_pre = sem("first_pre")
        bias_ready = sem("bias_ready")
        lstm_w_ready = sem("lstm_w_ready")
        rest_w_ready = sem("rest_w_ready")
        seg_sems = []

        def seg_sem(name):
            seg_sems.append(sem(name))
            return seg_sems[-1]

        lstm_h1_ready = seg_sem("lstm_h1_ready")
        lstm_hf_ready = seg_sem("lstm_hf_ready")
        lstm_h2_ready = seg_sem("lstm_h2_ready")
        lstm_pre_ready = seg_sem("lstm_pre_ready")
        lstm_sig_ready = seg_sem("lstm_sig_ready")
        lstm_g_ready = seg_sem("lstm_g_ready")
        lstm_fc_ready = seg_sem("lstm_fc_ready")
        lstm_c_ready = seg_sem("lstm_c_ready")
        lstm_tc_ready = seg_sem("lstm_tc_ready")
        gru_h1_ready = seg_sem("gru_h1_ready")
        gru_hf_ready = seg_sem("gru_hf_ready")
        gru_h2_ready = seg_sem("gru_h2_ready")
        gru_r_pre_ready = seg_sem("gru_r_pre_ready")
        gru_z_pre_ready = seg_sem("gru_z_pre_ready")
        gru_c_pre_ready = seg_sem("gru_c_pre_ready")
        gru_r_ready = seg_sem("gru_r_ready")
        gru_z_ready = seg_sem("gru_z_ready")
        gru_zc_ready = seg_sem("gru_zc_ready")
        gru_rh1_ready = seg_sem("gru_rh1_ready")
        gru_rhf_ready = seg_sem("gru_rhf_ready")
        gru_rh2_ready = seg_sem("gru_rh2_ready")
        gru_t_ready = seg_sem("gru_t_ready")
        xchunk_ready = seg_sem("xchunk_ready")
        xln_ready = seg_sem("xln_ready")
        q_pre_ready = seg_sem("q_pre_ready")
        k_pre_ready = seg_sem("k_pre_ready")
        v_pre_ready = seg_sem("v_pre_ready")
        q_ready = seg_sem("q_ready")
        k_ready = seg_sem("k_ready")
        v_ready = seg_sem("v_ready")
        s_pre_ready = seg_sem("s_pre_ready")
        s_ready = seg_sem("s_ready")
        o_ready = seg_sem("o_ready")
        ln_step = seg_sem("ln_step")
        var_ready = seg_sem("var_ready")
        rstd_ready = seg_sem("rstd_ready")
        x2_ready = seg_sem("x2_ready")
        x2T_ready = seg_sem("x2T_ready")
        x2_split = seg_sem("x2_split")
        x2p_ready = seg_sem("x2p_ready")
        keys_moved = seg_sem("keys_moved")
        values_moved = seg_sem("values_moved")
        lstm_in_used = seg_sem("lstm_in_used")
        hist_saved = seg_sem("hist_saved")
        seg_done = sem("seg_done")
        seg_clearing = sem("seg_clearing")
        seg_entered = sem("seg_entered")
        seg_go = sem("seg_go")
        logits_pre = sem("logits_pre")
        f_dve = sem("f_dve")
        exp_ready = sem("exp_ready")
        gates_ready = sem("gates_ready")
        gT_pre = sem("gT_pre")
        gT_ready = sem("gT_ready")
        acc0_pre = sem("acc0_pre")
        hid_pre = sem("hid_pre")
        hid_ready = sem("hid_ready")
        eo_pre = sem("eo_pre")
        acc_ready = sem("acc_ready")

        block = ctx.enter_context(nc.Block())

        def w(part, col):
            return wparts[:, part, col:col + D]

        def seg_end(eng, n):
            eng.drain().then_inc(seg_done, 1)
            eng.wait_ge(seg_go, n + 1)
            eng.sem_inc(seg_entered, 1)

        def lstm_place(i):
            return i // C, i % C

        def gru_place(i):
            t = i - C - LAG + SEG
            return t // C % 2, t % C

        def before(i):
            return i if i else SEG

        def attentions(first, last):
            return [(C, 0)] if first else [(0, -1)] if last else [(0, -1), (C, 0)]

        def gru_steps(first, last):
            return range(FIRST, SEG) if first else range(C + LAG) if last else range(SEG)

        @block.sync
        def _(sp):
            def load(dst, src, s):
                sp.dma_start(dst, src).then_inc(s, 16)

            load(wall[:, LX:LX + 4 * D], t_in["L0_cond_Wx"], lstm_w_in)
            load(wall[:, LH:LH + 4 * D], t_in["L0_cond_Wh"], lstm_w_in)
            load(wall[:, QKV:QKV + 3 * D], t_in["L0_attn_W_qkv"], rest_w_in)
            for g, n in enumerate(("L0_cond2_U_r", "L0_cond2_U_z", "L0_cond2_U")):
                load(wall[:, GH + g * D:GH + (g + 1) * D], t_in[n], rest_w_in)
            for g, n in enumerate(("L0_cond2_W_r", "L0_cond2_W_z", "L0_cond2_W")):
                load(wall[:, GX + g * D:GX + (g + 1) * D], t_in[n], rest_w_in)
            load(gate_w[:, :], t_in["L0_ffn_gate"], ffn_in)
            load(w1[:, :, :], t_in["L0_ffn_W1"].rearrange("e d h -> d e h"), ffn_in)
            load(w2[:, :, :, :], t_in["L0_ffn_W2"].rearrange("e (k p) d -> p e k d", p=128), ffn_in)
            sp.dma_start(b1[:, :, :], t_in["L0_ffn_b1"].rearrange("e (k p) -> p e k", p=128),
                         allow_slow_non_contiguous=True).then_inc(ffn_in, 16)
            load(b2[:, :], t_in["L0_ffn_b2"], ffn_in)

            def end_segment(n):
                sp.wait_ge(seg_done, 4 * (n + 1))
                sp.sem_inc(seg_clearing, 1)
                sp.sem_clear(range(seg_sems[0].num, seg_sems[-1].num + 1))
                sp.drain().then_inc(seg_go, 1)

            def save_x2(n, first, last):
                for k, (_, c) in enumerate(attentions(first, last)):
                    sp.wait_ge(x2_ready, k + 1)
                    sp.dma_start(x2_dram[bass.ds((2 * n + c) * R, R), :], x2rows[:, :]).then_inc(x2_saved, 16)

            save_x2(0, True, False)
            end_segment(0)
            with sp.Fori(1, NSEG) as n:
                save_x2(n, False, False)
                end_segment(n)
            save_x2(NSEG, False, True)
            sp.wait_ge(x2_saved, 16 * NCH)
            sp.dma_start(acc[:, :, :], x2_dram.rearrange("(k p) d -> p k d", p=128)).then_inc(x2_back, 16)
            end_segment(NSEG)
            steps = 128 // B
            for k in range(NT):
                sp.wait_ge(acc_ready, NE * NT + k + 1)
                for b in range(B):
                    sp.dma_start(out[b, k * steps:(k + 1) * steps, :], acc[b:128:B, k, :]).then_inc(stored, 16)
            sp.wait_ge(stored, 16 * NT * B)

        @block.gpsimd
        def _(pool):
            pool.memset(ident[:, :], 0.0).then_inc(pool_step, 1)
            pool.memset(batch_rows[:, :, :], 0.0).then_inc(pool_step, 1)
            pool.memset(onehot[:, :, :], 0.0).then_inc(pool_step, 1)
            pool.wait_ge(pool_step, 3)
            pool.affine_select(out=ident[:, :], in_=ident[:, :], compare_op=ALU.not_equal, fill=1.0, base=0,
                               pattern=[[-1, 128]], channel_multiplier=1).then_inc(ident_ready, 1)
            pool.affine_select(out=batch_rows[:, :, :], in_=batch_rows[:, :, :], compare_op=ALU.not_equal, fill=1.0,
                               base=0, pattern=[[0, 2 * C], [-1, B]], channel_multiplier=1).then_inc(batch_rows_ready, 1)
            for q in range(3):
                pool.affine_select(out=onehot[:, :, :], in_=onehot[:, :, :], compare_op=ALU.not_equal, fill=1.0,
                                   base=-32 * q, pattern=[[0, C], [-1, B]], channel_multiplier=1).then_inc(pool_step, 1)
                pool.wait_ge(pool_step, 4 + q)
            pool.memset(kT[:, 0:R], 0.0)
            pool.memset(vrows[0:R, :], 0.0)
            pool.memset(neghalf[:, :], -0.5)
            for p in range(PARTS_H):
                pool.memset(lstm_h[p][:, SEG, :], 0.0)
            for h in (gru_h1, gru_hf, gru_h2):
                pool.memset(h[:, 0:FIRST + 1, :], 0.0)
            pool.memset(xTparts[:, :, TOK:], 0.0)
            pool.memset(l_c[:, :], 0.0)
            pool.memset(l_g[:, :], 0.0)
            pool.memset(g_mul[:, :], 0.0)
            pool.memset(g_add[:, :], 0.0).then_inc(pool_step, 1)
            pool.wait_ge(pool_step, 7)
            pool.memset(g_add[:, 0:3 * B:3], HSCALE).then_inc(consts_ready, 1)
            pool.wait_ge(consts_ready, 1)
            pool.wait_ge(mask_same, 1)
            pool.affine_select(out=mask[0:R, :], in_=mask[0:R, :], compare_op=ALU.is_gt, fill=0.0, base=0,
                               pattern=[[-1, R]], channel_multiplier=1).then_inc(mask_ready, 1)
            pool.affine_select(out=mask[R:2 * R, :], in_=mask[R:2 * R, :], compare_op=ALU.is_ge, fill=0.0, base=0,
                               pattern=[[1, R]], channel_multiplier=-1).then_inc(mask_ready, 1)

            def segment(n, first, last):
                atts = attentions(first, last)

                def residual(k):
                    if k:
                        pool.wait_ge(x2_ready, k)
                    pool.tensor_tensor(xln[:, :], xrows[:, bass.ds(2 * n + atts[k][1], 1), :].rearrange("r n d -> r (n d)"),
                                       lnb[:, :], ALU.add).then_inc(xln_ready, 1)
                    pool.wait_ge(xln_ready, k + 1)

                def next_inputs(k):
                    if k:
                        pool.wait_ge(lstm_in_used, k)
                    pool.tensor_copy(xchunk[:, :, :], xTparts[:, :, bass.ds((2 * n + 1 + k) * R, R)]).then_inc(xchunk_ready, 1)

                def inv_std(k):
                    pool.wait_ge(var_ready, k + 1)
                    pool.tensor_tensor(rstd[:, :], var_eps[:, :], neghalf[:, :], ALU.pow).then_inc(rstd_ready, 1)
                    pool.wait_ge(rstd_ready, k + 1)

                def keep_states(lo, hi, token):
                    pool.tensor_copy(hist[:, bass.ds((token + LAG) * B, (hi - lo) * B)].rearrange("p (t b) -> p t b", b=B),
                                     gru_hf[:, lo + 1:hi + 1, 2:3 * B:3]).then_inc(hist_saved, 1)

                if not first:
                    keep_states(C, SEG, (n - 1) * SEG - LAG)
                if not last:
                    next_inputs(0)
                residual(0)
                inv_std(0)
                if not last:
                    if not first:
                        pool.wait_ge(gru_hf_ready, C)
                        keep_states(0, C, n * SEG - LAG - C)
                        residual(1)
                    next_inputs(1)
                    if not first:
                        inv_std(1)
                else:
                    pool.wait_ge(gru_hf_ready, C + LAG)
                    keep_states(0, C + LAG, n * SEG - LAG - C)
                seg_end(pool, n)

            pool.wait_ge(x_in, 16 * B)
            pool.wait_ge(small_in, 16 * SMALL)
            pool.wait_ge(xT_ready, 1)
            pool.wait_ge(mask_ready, 2)
            pool.wait_ge(first_pre, 1)
            segment(0, True, False)
            with pool.Fori(1, NSEG) as n:
                segment(n, False, False)
            segment(NSEG, False, True)

        @block.scalar
        def _(act):
            for b in range(B):
                act.dma_start(xrows[b:R:B, :, :], t_in["x"][b].rearrange("(n t) d -> t n d", t=C)).then_inc(x_in, 16)
            act.dma_start(condT[:, :], t_in["cond_1024"].rearrange("b d -> d b"),
                          allow_slow_non_contiguous=True).then_inc(cond_in, 16)
            for g, n in enumerate(("L0_cond2_C_r", "L0_cond2_C_z", "L0_cond2_C")):
                act.dma_start(cw[:, g * D:(g + 1) * D], t_in[n]).then_inc(cond_in, 16)
            n_small = 0

            def small(dst, src):
                act.dma_start(dst, src).then_inc(small_in, 16)
                return 1

            n_small += small(bias_in[:, 0:4 * D], t_in["L0_cond_b"].partition_broadcast(B))
            for g, n in enumerate(("L0_cond2_b_r", "L0_cond2_b_z", "L0_cond2_b")):
                n_small += small(bias_in[:, (4 + g) * D:(5 + g) * D], t_in[n].partition_broadcast(B))
            n_small += small(lnw[:, :], t_in["L0_attn_ln_w"].partition_broadcast(R))
            n_small += small(lnb[:, :], t_in["L0_attn_ln_b"].partition_broadcast(R))
            act.dma_start(bqk[:, :], t_in["L0_attn_b_qkv"][0:2 * D].rearrange("(k p) -> p k", p=128),
                          allow_slow_non_contiguous=True).then_inc(small_in, 16)
            n_small += 1
            n_small += small(bv[R:2 * R, :], t_in["L0_attn_b_qkv"][2 * D:3 * D].partition_broadcast(R))
            assert n_small == SMALL

            def query(k):
                act.wait_ge(q_pre_ready, k)
                act.activation(qT[:, :], p_a[:, 0:R], ACT.Identity, bias=bqk[:, 0:1]).then_inc(q_ready, 1)

            def move_keys(k):
                act.wait_ge(s_pre_ready, k)
                act.activation(kT[:, 0:R], kT[:, R:2 * R], ACT.Copy).then_inc(keys_moved, 1)

            def move_values(k):
                act.wait_ge(o_ready, k)
                act.activation(vrows[0:R, :], vrows[R:2 * R, :], ACT.Copy).then_inc(values_moved, 1)

            side = {1: query, 4: move_keys, 5: move_values}

            def segment(n, first, last):
                steps = gru_steps(first, last)
                starts = [a for a, _ in attentions(first, last)]
                for i in range(C + LAG if last else SEG):
                    for k, a in enumerate(starts):
                        if i - a in side:
                            side[i - a](k + 1)
                    if i in steps:
                        s = i - steps[0] + 1
                        c, t = gru_place(i)
                        act.wait_ge(gru_r_pre_ready, s)
                        act.activation(g_r[:, :], r_pre[c][:, t, :], ACT.Sigmoid).then_inc(gru_r_ready, 1)
                        act.wait_ge(gru_z_pre_ready, s)
                        act.activation(g_zc[:, :], zc_pre[c][:, t, 0, :], ACT.Sigmoid, scale=-1.0).then_inc(gru_zc_ready, 1)
                        act.activation(g_mul[:, 1:3 * B:3], zc_pre[c][:, t, 0, :], ACT.Sigmoid).then_inc(gru_z_ready, 1)
                    if not last:
                        c, t = lstm_place(i)
                        j = 4 * B * t
                        act.wait_ge(lstm_pre_ready, i + 1)
                        act.activation(l_gates[:, 0:6 * B:2], p_lstm[c][:, j:j + 3 * B], ACT.Sigmoid).then_inc(lstm_sig_ready, 1)
                        act.activation(l_g[:, 1:2 * B:2], p_lstm[c][:, j + 3 * B:j + 4 * B], ACT.Tanh).then_inc(lstm_g_ready, 1)
                    if i in steps:
                        c, t = gru_place(i)
                        act.wait_ge(gru_c_pre_ready, s)
                        act.activation(g_mul[:, 2:3 * B:3], zc_pre[c][:, t, 1, :], ACT.Tanh).then_inc(gru_t_ready, 1)
                    if not last:
                        act.wait_ge(lstm_c_ready, i + 1)
                        act.activation(l_tc[:, :], l_c[:, 1:2 * B:2], ACT.Tanh).then_inc(lstm_tc_ready, 1)
                seg_end(act, n)

            act.wait_ge(consts_ready, 1)
            act.wait_ge(small_in, 16 * SMALL)
            segment(0, True, False)
            with act.Fori(1, NSEG) as n:
                segment(n, False, False)
            segment(NSEG, False, True)

            act.wait_ge(ffn_in, 16 * 5)
            act.wait_ge(f_dve, 3)
            act.activation(logits[:, :, :], logits[:, :, :], ACT.Exp, scale=1.0 / HSCALE).then_inc(exp_ready, 1)
            i = 0
            for e in range(NE):
                for k in range(KH):
                    for h in range(TOK // HALF):
                        act.wait_ge(hid_pre, i + 1)
                        if e >= 2:
                            act.wait_ge(eo_pre, (e - 1) * NT)
                        act.activation(hidden[:, e % 2, k, h * HALF:(h + 1) * HALF], hid_bank[i % 4][:, :], ACT.Relu,
                                       bias=b1[:, e, k:k + 1], scale=1.0 / HSCALE).then_inc(hid_ready, 1)
                        i += 1

        @block.vector
        def _(dve):
            def link(ins, n=[0]):
                n[0] += 1
                ins.then_inc(dve_step, 1)
                dve.wait_ge(dve_step, n[0])

            def split3(parts, src, rest, scale=None):
                if scale is None:
                    link(dve.tensor_copy(parts[0], src))
                    link(dve.tensor_tensor(rest, src, parts[0], ALU.subtract))
                else:
                    link(dve.tensor_scalar(parts[0], src, scale, None, ALU.mult))
                    link(dve.scalar_tensor_tensor(out=rest, in0=src, scalar=scale, in1=parts[0],
                                                  op0=ALU.mult, op1=ALU.subtract))
                link(dve.tensor_copy(parts[1], rest))
                return dve.tensor_tensor(parts[2], rest, parts[1], ALU.subtract)

            def split_w(lo, hi, scale=None):
                return split3([wparts[:, p, lo:hi] for p in range(3)], wall[:, lo:hi], wrest[:, lo:hi], scale)

            link(dve.memset(bias_rows[:, :], 0.0))
            link(dve.memset(top[:, :, :], -1.0))
            dve.wait_ge(lstm_w_in, 32)
            split_w(LX, LX + 4 * D).then_inc(lstm_w_ready, 1)
            for h in range(TOK // HALF):
                dve.wait_ge(xT_pre, (h + 1) * (HALF // R))
                ins = split3([xTparts[:, p, h * HALF:(h + 1) * HALF] for p in range(3)], xT_bank[h][:, :],
                             xrest[:, h * HALF:(h + 1) * HALF])
                link(ins)
            link(dve.tensor_copy(xchunk[:, :, :], xTparts[:, :, 0:R]))
            dve.sem_inc(xT_ready, 1)
            split_w(LH, LH + 4 * D, 1.0 / HSCALE).then_inc(lstm_w_ready, 1)
            dve.wait_ge(small_in, 16 * SMALL)
            dve.wait_ge(vz_pre, 1)
            link(dve.tensor_copy(bias_sum[:, 0:4 * D], bias_in[:, 0:4 * D]))
            link(dve.tensor_tensor(bias_sum[:, 4 * D:7 * D], p_vz[0:B, 0:3 * D], bias_in[:, 4 * D:7 * D], ALU.add))
            link(dve.tensor_copy(bias_p[:, :], bias_sum[:, :]))
            link(dve.tensor_copy(bias_rows[0:B, :], bias_p[:, :]))
            link(dve.tensor_tensor(bias_rest[:, :], bias_sum[:, :], bias_p[:, :], ALU.subtract))
            link(dve.tensor_copy(bias_p[:, :], bias_rest[:, :]))
            link(dve.tensor_copy(bias_rows[32:32 + B, :], bias_p[:, :]))
            dve.tensor_tensor(bias_rows[64:64 + B, :], bias_rest[:, :], bias_p[:, :], ALU.subtract).then_inc(bias_ready, 1)
            dve.wait_ge(same_pre, 1)
            dve.tensor_scalar(mask[:, :], p_same[:, 0:R], SCORE_SCALE, None, ALU.mult).then_inc(mask_same, 1)
            dve.wait_ge(rest_w_in, 16 * 7)
            link(split_w(GH, NSTATE, 1.0 / HSCALE))
            split_w(GX, NW).then_inc(rest_w_ready, 1)
            dve.wait_ge(consts_ready, 1)
            dve.wait_ge(mask_ready, 2)

            def h_of(t, s):
                return t[:, s, 2:3 * B:3]

            def gru_gates(i, s):
                h = h_of(gru_hf, before(i))
                dve.wait_ge(gru_r_ready, s)
                dve.tensor_tensor(g_rh[0][:, :], g_r[:, :], h, ALU.mult).then_inc(gru_rh1_ready, 1)
                dve.tensor_tensor(g_rhf[:, :], g_r[:, :], h, ALU.mult).then_inc(gru_rhf_ready, 1)
                dve.wait_ge(gru_zc_ready, s)
                dve.tensor_tensor(g_add[:, 2:3 * B:3], g_zc[:, :], h, ALU.mult)
                dve.wait_ge(gru_rhf_ready, s)
                dve.tensor_tensor(g_rh[1][:, :], g_rhf[:, :], g_rh[0][:, :], ALU.subtract).then_inc(gru_rh2_ready, 1)

            def gru_state(i, s, kept):
                if kept and i == C:
                    dve.wait_ge(hist_saved, 1)
                dve.wait_ge(gru_t_ready, s)
                dve.tensor_tensor_scan(gru_h1[:, i + 1, :], g_mul[:, :], g_add[:, :], 0.0,
                                       ALU.mult, ALU.add).then_inc(gru_h1_ready, 1)
                dve.tensor_tensor_scan(gru_hf[:, i + 1, :], g_mul[:, :], g_add[:, :], 0.0,
                                       ALU.mult, ALU.add).then_inc(gru_hf_ready, 1)
                dve.wait_ge(gru_hf_ready, s)
                dve.tensor_tensor(gru_h2[:, i + 1, :], h_of(gru_hf, i + 1), h_of(gru_h1, i + 1),
                                  ALU.subtract).then_inc(gru_h2_ready, 1)

            def lstm_cell(i):
                dve.wait_ge(lstm_sig_ready, i + 1)
                dve.tensor_tensor(l_gates[:, 1:2 * B:2], l_gates[:, 2 * B:4 * B:2], l_c[:, 1:2 * B:2],
                                  ALU.mult).then_inc(lstm_fc_ready, 1)
                dve.wait_ge(lstm_fc_ready, i + 1)
                dve.wait_ge(lstm_g_ready, i + 1)
                dve.tensor_tensor_scan(l_c[:, :], l_g[:, :], l_gates[:, 0:2 * B], 0.0,
                                       ALU.mult, ALU.add).then_inc(lstm_c_ready, 1)

            def lstm_state(i):
                o = l_gates[:, 4 * B:6 * B:2]
                dve.wait_ge(lstm_tc_ready, i + 1)
                dve.scalar_tensor_tensor(out=lstm_h[0][:, i + 1, :], in0=o, scalar=HSCALE, in1=l_tc[:, :],
                                         op0=ALU.mult, op1=ALU.mult).then_inc(lstm_h1_ready, 1)
                dve.scalar_tensor_tensor(out=lstm_hf[:, i % 2, :], in0=o, scalar=HSCALE, in1=l_tc[:, :],
                                         op0=ALU.mult, op1=ALU.mult).then_inc(lstm_hf_ready, 1)
                dve.wait_ge(lstm_hf_ready, i + 1)
                dve.tensor_tensor(lstm_h[1][:, i + 1, :], lstm_hf[:, i % 2, :], lstm_h[0][:, i + 1, :],
                                  ALU.subtract).then_inc(lstm_h2_ready, 1)

            def keys(k, saved):
                if k > 1:
                    dve.wait_ge(keys_moved, k - 1)
                dve.wait_ge(k_pre_ready, k)
                dve.tensor_scalar(kT[:, R:2 * R], p_b[:, 0:R], bqk[:, 1:2], None, ALU.add).then_inc(k_ready, 1)

            def values(k, saved):
                if k > 1:
                    dve.wait_ge(values_moved, k - 1)
                dve.wait_ge(v_pre_ready, k)
                dve.tensor_tensor(vrows[R:2 * R, :], p_a[R:2 * R, 0:D], bv[R:2 * R, :], ALU.add).then_inc(v_ready, 1)

            def masked_scores(k, saved):
                dve.wait_ge(s_pre_ready, k)
                dve.tensor_tensor(sT[:, :], p_b[:, 0:R], mask[:, :], ALU.mult).then_inc(s_ready, 1)

            def ln_stats(k, saved):
                dve.wait_ge(o_ready, k)
                dve.bn_stats(stats[:, :], p_b[0:R, 0:D]).then_inc(ln_step, 1)

            def ln_variance(k, saved):
                dve.wait_ge(ln_step, 3 * k - 2)
                dve.bn_aggr(aggr[:, :], stats[:, :]).then_inc(ln_step, 1)

            def ln_centre(k, saved):
                dve.wait_ge(ln_step, 3 * k - 1)
                dve.tensor_scalar(var_eps[:, :], aggr[:, 1:2], LN_EPS, None, ALU.add).then_inc(var_ready, 1)
                dve.scalar_tensor_tensor(out=centred[:, :], in0=p_b[0:R, 0:D], scalar=aggr[:, 0:1], in1=lnw[:, :],
                                         op0=ALU.subtract, op1=ALU.mult).then_inc(ln_step, 1)

            def residual(k, saved):
                dve.wait_ge(ln_step, 3 * k)
                dve.wait_ge(rstd_ready, k)
                dve.wait_ge(xln_ready, k)
                if saved is not None:
                    dve.wait_ge(x2_saved, saved)
                dve.scalar_tensor_tensor(out=x2rows[:, :], in0=centred[:, :], scalar=rstd[:, 0:1], in1=xln[:, :],
                                         op0=ALU.mult, op1=ALU.add).then_inc(x2_ready, 1)

            def split_a(k, saved):
                dve.wait_ge(x2T_ready, k)
                dve.tensor_copy(x2parts[0][:, :], p_a[:, 0:R]).then_inc(x2p_ready, 1)

            def split_b(k, saved):
                dve.wait_ge(x2p_ready, 3 * k - 2)
                dve.tensor_tensor(x2rest[:, :], p_a[:, 0:R], x2parts[0][:, :], ALU.subtract).then_inc(x2_split, 1)

            def split_c(k, saved):
                dve.wait_ge(x2_split, k)
                dve.tensor_copy(x2parts[1][:, :], x2rest[:, :]).then_inc(x2p_ready, 1)

            def split_d(k, saved):
                dve.wait_ge(x2p_ready, 3 * k - 1)
                dve.tensor_tensor(x2parts[2][:, :], x2rest[:, :], x2parts[1][:, :], ALU.subtract).then_inc(x2p_ready, 1)

            side = {1: [keys], 2: [values], 3: [masked_scores], 4: [ln_stats], 5: [ln_variance], 6: [ln_centre],
                    7: [residual], 8: [split_a], 9: [split_b, split_c], 10: [split_d]}

            def segment(n, first, last):
                steps = gru_steps(first, last)
                atts = attentions(first, last)
                kept = not first
                for i in range(C + LAG if last else SEG):
                    for k, (a, c) in enumerate(atts):
                        for piece in side.get(i - a, []):
                            piece(k + 1, None if first else 16 * (2 * n + c))
                    if i in steps:
                        gru_gates(i, i - steps[0] + 1)
                    if not last:
                        lstm_cell(i)
                    if i in steps:
                        gru_state(i, i - steps[0] + 1, kept)
                    if not last:
                        lstm_state(i)
                seg_end(dve, n)

            segment(0, True, False)
            with dve.Fori(1, NSEG) as n:
                segment(n, False, False)
            segment(NSEG, False, True)

            lg = p_a[:, 0:NT * NE].rearrange("p (k e) -> p k e", e=NE)

            def over_experts(x):
                return x[:, :].unsqueeze(2).broadcast_to([128, NT, NE])

            def fstep(ins, n=[0]):
                n[0] += 1
                ins.then_inc(f_dve, 1)
                dve.wait_ge(f_dve, n[0])

            dve.wait_ge(logits_pre, 1)
            fstep(dve.tensor_copy(raw_gate[:, :, :], lg))
            fstep(dve.tensor_reduce(row_a[:, :], raw_gate[:, :, :], AX.X, ALU.max))
            fstep(dve.tensor_tensor(logits[:, :, :], raw_gate[:, :, :], over_experts(row_a), ALU.subtract))
            dve.wait_ge(exp_ready, 1)
            fstep(dve.tensor_reduce(row_a[:, :], logits[:, :, :], AX.X, ALU.add))
            fstep(dve.reciprocal(row_b[:, :], row_a[:, :]))
            fstep(dve.tensor_tensor(raw_gate[:, :, :], logits[:, :, :], over_experts(row_b), ALU.mult))
            for k in range(NT):
                ins = dve.max(logits[:, k, :], raw_gate[:, k, :])
            fstep(ins)
            fstep(dve.tensor_copy(top[:, :, 0:2], logits[:, :, 0:2]))
            for k in range(NT):
                ins = dve.match_replace(struck[:, k, :], top[:, k, :], raw_gate[:, k, :], -2.0)
            fstep(ins)
            fstep(dve.scalar_tensor_tensor(out=gates[:, :, :], in0=struck[:, :, :], scalar=0.0, in1=raw_gate[:, :, :],
                                           op0=ALU.is_lt, op1=ALU.mult))
            fstep(dve.tensor_reduce(row_a[:, :], gates[:, :, :], AX.X, ALU.add))
            fstep(dve.tensor_scalar(row_a[:, :], row_a[:, :], 1e-12, None, ALU.max))
            fstep(dve.reciprocal(row_b[:, :], row_a[:, :]))
            dve.tensor_tensor(gates[:, :, :], gates[:, :, :], over_experts(row_b), ALU.mult).then_inc(gates_ready, 1)
            for h in range(TOK // HALF):
                dve.wait_ge(gT_pre, h + 1)
                dve.tensor_copy(gates_T[:, h * HALF:(h + 1) * HALF], gT_bank[h][0:NE, :]).then_inc(gT_ready, 1)
            dve.wait_ge(x2_back, 16)
            for k in range(NT):
                dve.wait_ge(acc0_pre, k // 4 * 4 + 4)
                dve.tensor_tensor(acc[:, k, :], eo_bank[k // 4][:, k % 4 * D:(k % 4 + 1) * D], acc[:, k, :],
                                  ALU.add).then_inc(acc_ready, 1)
            dve.wait_ge(gates_ready, 1)
            for e in range(NE):
                for k in range(NT):
                    dve.wait_ge(eo_pre, e * NT + k // 4 * 4 + 4)
                    dve.wait_ge(acc_ready, e * NT + k + 1)
                    dve.scalar_tensor_tensor(out=acc[:, k, :], in0=eo_bank[k // 4][:, k % 4 * D:(k % 4 + 1) * D],
                                             scalar=gates[:, k, e:e + 1], in1=acc[:, k, :],
                                             op0=ALU.mult, op1=ALU.add).then_inc(acc_ready, 1)

        @block.tensor
        def _(pe):
            def mm(out_, lhsT, rhs, start=False):
                return pe.matmul(out_, lhsT, rhs, start=start, stop=True, skip_group_check=True)

            def by_step(x):
                return x.rearrange("p (t b) -> p t b", b=B)

            def lstm_from_x(c, g):
                mm(lstm_pre[c][:, :, g, :], bias_rows[:, g * D:(g + 1) * D], onehot[:, :, :], start=(g == 0))
                for a, b in PROD_X:
                    ins = mm(lstm_pre[c][:, :, g, :], w(a, LX + g * D), by_step(xchunk[:, b, :]))
                return ins

            def gru_outs(c):
                return [r_pre[c], zc_pre[c][:, :, 0, :], zc_pre[c][:, :, 1, :]]

            pe.wait_ge(ident_ready, 1)
            pe.wait_ge(x_in, 16 * B)
            for n in range(NCH):
                h, j = n * R // HALF, n * R % HALF
                pe.transpose(xT_bank[h][:, j:j + R], xrows[:, n, :], ident[0:R, 0:R]).then_inc(xT_pre, 1)
            pe.wait_ge(cond_in, 16 * 4)
            mm(p_vz[0:B, 0:3 * D], condT[:, :], cw[:, :], start=True).then_inc(vz_pre, 1)
            pe.wait_ge(batch_rows_ready, 1)
            batches = batch_rows[:, :, :].rearrange("p t b -> p (t b)")
            mm(p_same[:, 0:R], batches, batches[:, 0:R], start=True).then_inc(same_pre, 1)
            pe.wait_ge(bias_ready, 1)
            pe.wait_ge(consts_ready, 1)
            pe.wait_ge(lstm_w_ready, 2)
            pe.wait_ge(xT_ready, 1)
            for g in range(4):
                lstm_from_x(0, g)
            for g in range(4):
                ins = mm(lstm_pre[0][:, 0, g, :], wall[:, LH + g * D:LH + (g + 1) * D], condT[:, :])
            ins.then_inc(first_pre, 1)
            pe.wait_ge(rest_w_ready, 1)

            def lstm_products(i, pairs):
                c, t = lstm_place(i)
                for g in range(4):
                    for a, b in pairs:
                        ins = mm(lstm_pre[c][:, t, g, :], w(a, LH + g * D), lstm_h[b][:, before(i), :])
                return ins

            def gru_products(i, g, pairs):
                c, t = gru_place(i)
                h = [gru_h1[:, before(i), 2:3 * B:3], gru_h2[:, before(i), :]] if g < 2 else [x[:, :] for x in g_rh]
                for a, b in pairs:
                    ins = mm(gru_outs(c)[g][:, t, :], w(a, GH + g * D), h[b])
                return ins

            pairs = PROD_FIRST + PROD_SECOND

            def states(c):
                lo = 1 if c == 0 else 1 + C
                return [lstm_h[p][:, lo:lo + C, :].rearrange("p t b -> p (t b)") for p in range(PARTS_H)]

            def queries_keys(k, c):
                for j, (out_, done) in enumerate(((p_a, q_pre_ready), (p_b, k_pre_ready))):
                    for m, (a, b) in enumerate(pairs):
                        ins = mm(out_[:, 0:R], w(a, QKV + j * D), states(c)[b], start=(m == 0))
                    ins.then_inc(done, 1)

            def values(k, c):
                pe.wait_ge(q_ready, k)
                for m, (a, b) in enumerate(pairs):
                    ins = mm(p_a[R:2 * R, 0:D], states(c)[b], w(a, QKV + 2 * D), start=(m == 0))
                ins.then_inc(v_pre_ready, 1)

            def scores(k, c):
                pe.wait_ge(k_ready, k)
                mm(p_b[:, 0:R], kT[:, :], qT[:, :], start=True).then_inc(s_pre_ready, 1)

            def output(k, c):
                pe.wait_ge(s_ready, k)
                pe.wait_ge(v_ready, k)
                mm(p_b[0:R, 0:D], sT[:, :], vrows[:, :], start=True).then_inc(o_ready, 1)

            def columns(k, c):
                pe.wait_ge(x2_ready, k)
                pe.transpose(p_a[:, 0:R], x2rows[:, :], ident[0:R, 0:R]).then_inc(x2T_ready, 1)

            def gru_from_x(part):
                def piece(k, c):
                    outs = gru_outs(c % 2)
                    if part == 0:
                        for g in range(3):
                            mm(outs[g], bias_rows[:, (4 + g) * D:(5 + g) * D], onehot[:, :, :], start=(g < 2))
                    pe.wait_ge(x2p_ready, 3 * (k - 1) + part + 1)
                    for g in range(3):
                        for a in range(3 - part):
                            mm(outs[g], w(a, GX + g * D), by_step(x2parts[part][:, :]))
                return piece

            side = {0: queries_keys, 1: values, 2: scores, 3: output, 7: columns, 8: gru_from_x(0), 9: gru_from_x(1),
                    10: gru_from_x(2)}
            AHEAD = 16

            def segment(n, first, last):
                steps = gru_steps(first, last)
                atts = attentions(first, last)
                for i in range(C + LAG if last else SEG):
                    s = i - steps[0]
                    if i in steps:
                        if s:
                            pe.wait_ge(gru_h1_ready, s)
                        gru_products(i, 0, PROD_FIRST)
                        gru_products(i, 1, PROD_FIRST)
                        if s:
                            pe.wait_ge(gru_h2_ready, s)
                        gru_products(i, 0, PROD_SECOND).then_inc(gru_r_pre_ready, 1)
                        gru_products(i, 1, PROD_SECOND).then_inc(gru_z_pre_ready, 1)
                    if not last:
                        if i:
                            pe.wait_ge(lstm_h1_ready, i)
                        lstm_products(i, PROD_FIRST)
                        if i:
                            pe.wait_ge(lstm_h2_ready, i)
                        lstm_products(i, PROD_SECOND).then_inc(lstm_pre_ready, 1)
                    if i in steps:
                        pe.wait_ge(gru_rh1_ready, s + 1)
                        pe.wait_ge(gru_z_ready, s + 1)
                        gru_products(i, 2, PROD_FIRST)
                        pe.wait_ge(gru_rh2_ready, s + 1)
                        gru_products(i, 2, PROD_SECOND).then_inc(gru_c_pre_ready, 1)
                    for k, (a, c) in enumerate(atts):
                        if i - a in side:
                            side[i - a](k + 1, c)
                    if not last and AHEAD <= i % C < AHEAD + 4:
                        k, g = i // C + 1, i % C - AHEAD
                        pe.wait_ge(xchunk_ready, k)
                        ins = lstm_from_x(k % 2, g)
                        if g == 3:
                            ins.then_inc(lstm_in_used, 1)
                seg_end(pe, n)

            segment(0, True, False)
            with pe.Fori(1, NSEG) as n:
                segment(n, False, False)
            segment(NSEG, False, True)

            pe.wait_ge(ffn_in, 16 * 5)
            for k in range(NT):
                ins = mm(p_a[:, k * NE:(k + 1) * NE], hT[:, k * 128:(k + 1) * 128], gate_w[:, :], start=(k == 0))
            ins.then_inc(logits_pre, 1)

            def hidden_rows(e):
                i = e * KH * (TOK // HALF)
                for k in range(KH):
                    for h in range(TOK // HALF):
                        if i >= 4:
                            pe.wait_ge(hid_ready, i - 3)
                        mm(hid_bank[i % 4][:, :], w1[:, e, k * 128:(k + 1) * 128], hT[:, h * HALF:(h + 1) * HALF],
                           start=True).then_inc(hid_pre, 1)
                        i += 1

            def expert_out(e):
                pe.wait_ge(hid_ready, (e + 1) * KH * (TOK // HALF))
                for k in range(NT):
                    if k % 4 == 0:
                        pe.wait_ge(acc_ready, e * NT + k + 4)
                    for j in range(KH):
                        ins = mm(eo_bank[k // 4][:, k % 4 * D:(k % 4 + 1) * D], hidden[:, e % 2, j, k * 128:(k + 1) * 128],
                                 w2[:, e, j, :], start=(k % 4 == 0 and j == 0))
                    ins.then_inc(eo_pre, 1)

            hidden_rows(0)
            pe.wait_ge(gates_ready, 1)
            for k in range(NT):
                h, j = divmod(k * 128, HALF)
                ins = pe.transpose(gT_bank[h][0:NE, j:j + 128], gates[:, k, :], ident[:, :])
                if k % 4 == 3:
                    ins.then_inc(gT_pre, 1)
            for k in range(NT):
                pe.wait_ge(gT_ready, k // 4 + 1)
                mm(eo_bank[k // 4][:, k % 4 * D:(k % 4 + 1) * D], gates_T[:, k * 128:(k + 1) * 128], b2[:, :],
                   start=(k % 4 == 0)).then_inc(acc0_pre, 1)
            for e in range(NE):
                if e + 1 < NE:
                    hidden_rows(e + 1)
                expert_out(e)


_INS = ["x", "cond_1024", "L0_cond_Wx", "L0_cond_Wh", "L0_cond_b", "L0_attn_W_qkv", "L0_attn_b_qkv",
        "L0_attn_ln_w", "L0_attn_ln_b", "L0_cond2_W_z", "L0_cond2_U_z", "L0_cond2_C_z", "L0_cond2_b_z",
        "L0_cond2_W_r", "L0_cond2_U_r", "L0_cond2_C_r", "L0_cond2_b_r", "L0_cond2_W", "L0_cond2_U",
        "L0_cond2_C", "L0_cond2_b", "L0_ffn_gate", "L0_ffn_W1", "L0_ffn_b1", "L0_ffn_W2", "L0_ffn_b2"]


def kernel(**inputs):
    import numpy as _np
    import concourse.bacc as _bacc
    from concourse import mybir as _mybir
    from concourse.bass_utils import run_bass_kernel_spmd as _run

    nc = _bacc.Bacc("TRN2", target_bir_lowering=False, num_devices=1)
    arrays, t_in = {}, {}
    for name in _INS:
        a = _np.ascontiguousarray(inputs[name])
        arrays[f"in_{name}"] = a
        t_in[name] = nc.dram_tensor(f"in_{name}", a.shape, _mybir.dt.from_np(a.dtype), kind="ExternalInput").ap()
    out = nc.dram_tensor("out_0", inputs["x"].shape, _mybir.dt.float32, kind="ExternalOutput").ap()
    adaln_kernel(nc, t_in, out)
    r = _run(nc, [arrays], core_ids=[0])
    return r.results[0]["out_0"]
```

```python
from contextlib import ExitStack

import concourse.bass as bass
from concourse import mybir

F32 = mybir.dt.float32
BF16 = mybir.dt.bfloat16
FP16 = mybir.dt.float16
ALU = mybir.AluOpType
ACT = mybir.ActivationFunctionType
AX = mybir.AxisListType

D = 128
SPAN = 32
LN_EPS = 1e-5
NE, HID = 8, 256
EULER = 2.718281828459045
HSCALE = 4096.0
GRID = 1.5 * 2.0 ** 24
PARTS_W, PARTS_H = 3, 2
PROD_FIRST = [(2, 0), (1, 0), (0, 0)]
PROD_SECOND = [(1, 1), (0, 1)]
PROD_X = [(2, 0), (1, 1), (0, 2), (1, 0), (0, 1), (0, 0)]


def adaln_kernel(nc: bass.Bass, t_in, out: bass.AP):
    B, T, _ = t_in["x"].shape
    C = SPAN
    NCH = T // C
    SEG = 2 * C
    NSEG = T // SEG
    LAG = 9
    FIRST = C + LAG
    R = C * B
    TOK = T * B
    NT = TOK // 128
    TILE = 128 // B
    KH = HID // 128
    HALF = 512
    assert TILE == SEG and KH == 2

    LH = 0
    GH = LH + 4 * D
    QKV = GH + 3 * D
    NSTATE = QKV + 3 * D
    LX = NSTATE
    GX = LX + 4 * D
    NW = GX + 3 * D
    SCORE_SCALE = 1.0 / float(D * SPAN) ** 0.5

    with ExitStack() as ctx:
        def sb(name, shape, dt=F32):
            return ctx.enter_context(nc.sbuf_tensor(name, shape, dt))

        def pb(name, shape=(128, 512)):
            return ctx.enter_context(nc.psum_tensor(name, list(shape), F32))

        def sem(name):
            return ctx.enter_context(nc.semaphore(name))

        wall = sb("wall", [128, NW])
        wrest = sb("wrest", [128, NW])
        wparts = sb("wparts", [128, PARTS_W, NW], BF16)
        cw = sb("cw", [128, 3 * D])
        condT = sb("condT", [128, B])
        xrows = sb("xrows", [R, NCH, D])
        xrest = sb("xrest", [128, TOK])
        xTparts = sb("xTparts", [128, 3, TOK + R], BF16)
        xchunk = sb("xchunk", [128, 3, R], BF16)
        ident = sb("ident", [128, 128])
        lnw = sb("lnw", [R, D])
        lnb = sb("lnb", [R, D])
        bqk = sb("bqk", [128, 2])
        bv = sb("bv", [2 * R, D])
        GROUPS = 3 * 32
        condT3 = sb("condT3", [128, 3, 32])
        bias_in = sb("bias_in", [GROUPS, 7 * D])
        bias_sum = sb("bias_sum", [GROUPS, 3 * D])
        bias_rest = sb("bias_rest", [GROUPS, 7 * D])
        bias_rows = sb("bias_rows", [128, 7 * D], BF16)
        warm = sb("warm", [1, 1])
        onehot = sb("onehot", [128, C, B], BF16)
        batch_rows = sb("batch_rows", [B, C * 2, B])
        mask = sb("mask", [128, R])
        neghalf = sb("neghalf", [R, 1])

        lstm_h = [sb(f"lstm_h{p}", [128, SEG + 1, B, 3], FP16) for p in range(PARTS_H)]
        l_gates = sb("l_gates", [128, 3, B, 3])
        l_g = sb("l_g", [128, B, 3])
        l_c = sb("l_c", [128, B, 3])

        g_add = sb("g_add", [128, B, 6])
        gru_h1 = sb("gru_h1", [128, B, 6], FP16)
        gru_hf = sb("gru_hf", [128, SEG + 1, B, 6])
        gru_h2 = sb("gru_h2", [128, B], FP16)
        wneg = sb("wneg", [128, 2, 2 * D], BF16)
        g_zc = sb("g_zc", [128, B])
        g_rh1 = sb("g_rh1", [128, B, 6], FP16)
        g_rh2 = sb("g_rh2", [128, B, 6], FP16)

        qT = sb("qT", [128, R])
        kT = sb("kT", [128, 2 * R])
        vrows = sb("vrows", [2 * R, D])
        sT = sb("sT", [2 * R, R])
        stats = sb("stats", [R, 6])
        aggr = sb("aggr", [R, 2])
        var_eps = sb("var_eps", [R, 1])
        rstd = sb("rstd", [R, 1])
        centred = sb("centred", [R, D])
        xln = sb("xln", [R, D])
        x2rows = sb("x2rows", [R, D])
        x2parts = [sb(f"x2parts{p}", [128, R], BF16) for p in range(3)]
        x2rest = sb("x2rest", [128, R])
        gathered = sb("gathered", [128, TILE, B])
        tile_h = sb("tile_h", [128, 128])

        gate_w = sb("gate_w", [128, NE])
        w1 = sb("w1", [128, NE, HID])
        w2 = sb("w2", [128, NE, KH, D])
        b1 = sb("b1", [128, NE, KH])
        b2 = sb("b2", [NE, D])
        logits = sb("logits", [128, NE])
        largest = sb("largest", [128, 8])
        expo = sb("expo", [128, NE])
        euler = sb("euler", [128, NE])
        exps = sb("exps", [128, NE])
        probs = sb("probs", [128, NE])
        top = sb("top", [128, 8])
        struck = sb("struck", [128, NE])
        chosen = sb("chosen", [128, NE])
        row_sum = sb("row_sum", [128, 1])
        row_inv = sb("row_inv", [128, 1])
        gates = sb("gates", [128, NE])
        gates_T = sb("gates_T", [NE, 128])
        hidden = sb("hidden", [128, KH, 128])
        tail_hidden = sb("tail_hidden", [128, NE, KH, 128])
        acc = sb("acc", [128, D])
        x2all = sb("x2all", [128, NT + 1, D])

        p_lstm = [pb(f"p_lstm{c}") for c in range(2)]
        p_rg = [pb(f"p_rg{c}") for c in range(2)]
        p_zc = [pb(f"p_zc{c}") for c in range(2)]
        p_a = pb("p_a")
        p_b = pb("p_b")
        ifo_pre = [p[:, 0:3 * R].rearrange("p (t g b) -> p t g b", g=3, b=B) for p in p_lstm]
        r_pre = [p[:, 0:R].rearrange("p (t b) -> p t b", b=B) for p in p_rg]
        g_pre = [p[:, R:2 * R].rearrange("p (t b) -> p t b", b=B) for p in p_rg]

        LATE = HALF // 2
        g_mul = [p[:, LATE:LATE + 6 * B].rearrange("p (b k) -> p b k", k=6) for p in p_zc]
        r_out = [p_zc[1 - c][:, LATE + 6 * B:LATE + 7 * B] for c in range(2)]

        def lstm_pre(c, g):
            return g_pre[c] if g == 3 else ifo_pre[c][:, :, g, :]

        zc_pre = [p[:, 0:2 * R].rearrange("p (t g b) -> p t g b", g=2, b=B) for p in p_zc]

        xT_bank = [p_a, p_b]
        p_vz, p_same = p_rg[1], p_zc[1]
        def expert_banks(last):
            return (p_lstm[0], p_lstm[1]) if last else (p_a, p_b)

        tail_banks = p_lstm + p_rg

        def tail_out(e):
            j = e * D if e < 4 else (e - 4) * D if e < NE - 1 else 0
            return (p_zc[0] if e < 4 else p_zc[1] if e < NE - 1 else p_b)[:, j:j + D]

        def tail_out_complete(e):
            return 4 if e < 4 else NE - 1 if e < NE - 1 else NE

        lstm_wx_in = sem("lstm_wx_in")
        lstm_wh_in = sem("lstm_wh_in")
        rest_w_in = sem("rest_w_in")
        cond_in = sem("cond_in")
        small_in = sem("small_in")
        lstm_b_in = sem("lstm_b_in")
        gru_b_in = sem("gru_b_in")
        SMALL = 4
        x_in = sem("x_in")
        ffn_in = sem("ffn_in")
        x2_saved = sem("x2_saved")
        stored = sem("stored")
        pool_step = sem("pool_step")
        dve_step = sem("dve_step")
        ident_ready = sem("ident_ready")
        batch_rows_ready = sem("batch_rows_ready")
        consts_ready = sem("consts_ready")
        same_pre = sem("same_pre")
        mask_same = sem("mask_same")
        mask_ready = sem("mask_ready")
        xT_pre = sem("xT_pre")
        vz_ready = sem("vz_ready")
        setup_step = sem("setup_step")
        vz_pre = sem("vz_pre")
        first_pre = sem("first_pre")
        cond3_ready = sem("cond3_ready")
        bias_rows_zero = sem("bias_rows_zero")
        bias_step = sem("bias_step")
        xchunk_first = sem("xchunk_first")
        lstm_w_ready = sem("lstm_w_ready")
        seg_sems = []

        def seg_sem(name):
            seg_sems.append(sem(name))
            return seg_sems[-1]

        lstm_h1_ready = seg_sem("lstm_h1_ready")
        lstm_h2_ready = seg_sem("lstm_h2_ready")
        lstm_ifo_pre_ready = seg_sem("lstm_ifo_pre_ready")
        lstm_g_pre_ready = seg_sem("lstm_g_pre_ready")
        lstm_sig_ready = seg_sem("lstm_sig_ready")
        lstm_g_ready = seg_sem("lstm_g_ready")
        lstm_fc_ready = seg_sem("lstm_fc_ready")
        lstm_c_ready = seg_sem("lstm_c_ready")
        lstm_tc_ready = seg_sem("lstm_tc_ready")
        gru_h1_ready = seg_sem("gru_h1_ready")
        gru_hf_ready = seg_sem("gru_hf_ready")
        gru_h2_ready = seg_sem("gru_h2_ready")
        gru_r_pre_ready = seg_sem("gru_r_pre_ready")
        gru_z_pre_ready = seg_sem("gru_z_pre_ready")
        gru_c_pre_ready = seg_sem("gru_c_pre_ready")
        gru_r_ready = seg_sem("gru_r_ready")
        gru_r_again_ready = seg_sem("gru_r_again_ready")
        gru_z_ready = seg_sem("gru_z_ready")
        gru_zc_ready = seg_sem("gru_zc_ready")
        gru_rh1_ready = seg_sem("gru_rh1_ready")
        gru_rh2_ready = seg_sem("gru_rh2_ready")
        gru_kept_ready = seg_sem("gru_kept_ready")
        gru_t_ready = seg_sem("gru_t_ready")
        xchunk_ready = seg_sem("xchunk_ready")
        xln_ready = seg_sem("xln_ready")
        q_pre_ready = seg_sem("q_pre_ready")
        k_pre_ready = seg_sem("k_pre_ready")
        v_pre_ready = seg_sem("v_pre_ready")
        q_ready = seg_sem("q_ready")
        k_ready = seg_sem("k_ready")
        v_ready = seg_sem("v_ready")
        s_pre_ready = seg_sem("s_pre_ready")
        s_ready = seg_sem("s_ready")
        o_ready = seg_sem("o_ready")
        ln_step = seg_sem("ln_step")
        var_ready = seg_sem("var_ready")
        rstd_ready = seg_sem("rstd_ready")
        x2_ready = seg_sem("x2_ready")
        x2T_ready = seg_sem("x2T_ready")
        x2_split = seg_sem("x2_split")
        x2p_ready = seg_sem("x2p_ready")
        keys_moved = seg_sem("keys_moved")
        values_moved = seg_sem("values_moved")
        lstm_in_used = seg_sem("lstm_in_used")
        tile_moved = seg_sem("tile_moved")
        gathering = seg_sem("gathering")
        logits_ready = seg_sem("logits_ready")
        gate_step = seg_sem("gate_step")
        exps_ready = seg_sem("exps_ready")
        gT_pre = seg_sem("gT_pre")
        gT_ready = seg_sem("gT_ready")
        hid_pre = seg_sem("hid_pre")
        hid_ready = seg_sem("hid_ready")
        eo_pre = seg_sem("eo_pre")
        acc_in = seg_sem("acc_in")
        acc_ready = seg_sem("acc_ready")
        acc_saved = seg_sem("acc_saved")
        seg_done = sem("seg_done")
        seg_clearing = sem("seg_clearing")
        seg_entered = sem("seg_entered")
        seg_go = sem("seg_go")
        tail_logits_ready = sem("tail_logits_ready")
        tail_gate_step = sem("tail_gate_step")
        tail_exps_ready = sem("tail_exps_ready")
        tail_gT_pre = sem("tail_gT_pre")
        tail_gT_ready = sem("tail_gT_ready")
        tail_hid_pre = sem("tail_hid_pre")
        tail_hid_ready = sem("tail_hid_ready")
        tail_bias_pre = sem("tail_bias_pre")
        tail_eo_pre = sem("tail_eo_pre")
        tail_acc_ready = sem("tail_acc_ready")

        SETUP_LATER = 2 * 4 + 3 * 4 + 1

        block = ctx.enter_context(nc.Block())

        def w(part, col):
            return wparts[:, part, col:col + D]

        def seg_end(eng):
            eng.drain().then_inc(seg_done, 1)

        def seg_begin(eng, n, first):
            if not first:
                eng.wait_ge(seg_go, n)
                eng.sem_inc(seg_entered, 1)

        def lstm_place(i):
            return i // C, i % C

        def gru_place(i):
            t = i - C - LAG + SEG
            return t // C % 2, t % C

        def before(i):
            return i if i else SEG

        def attentions(first, last):
            return [(C, 0)] if first else [(0, -1)] if last else [(0, -1), (C, 0)]

        def gru_steps(first, last):
            return range(FIRST, SEG) if first else range(C + LAG) if last else range(SEG)

        def expert_work(first, last):
            if first:
                return {}
            work = [("gates", 0, 0), ("bias", 0, 0)]
            for e in range(NE):
                work += [("hidden", e, j) for j in range(KH)] + [("out", e, j) for j in range(KH)]
            if last:
                steps = [i for i in range(1, C + LAG) if i not in (2, 3, 6, 7, 8)]
            else:
                steps = list(range(LAG + 1, C)) + list(range(C + LAG + 2, SEG))
            return dict(zip(steps, work))

        LOGITS = C + LAG + 1
        GATE_STEPS = {i: j for j, i in enumerate(list(range(LOGITS + 1, LOGITS + 4)) +
                                                 [i for i in range(LOGITS + 4, SEG) if i % 4 != 3][:11])}

        def bias_parts(eng, src, lo, hi, done):
            rows, rest = bias_rows[0:GROUPS, lo:hi], bias_rest[:, lo:hi]
            eng.tensor_copy(rows, src).then_inc(bias_step, 1)
            eng.wait_ge(bias_step, done + 1)
            eng.tensor_tensor(rest, src, rows, ALU.subtract).then_inc(bias_step, 1)
            eng.wait_ge(bias_step, done + 2)
            eng.tensor_copy(bias_rows[0:64, lo:hi], rest[0:64]).then_inc(bias_step, 1)
            eng.wait_ge(bias_step, done + 3)
            eng.tensor_tensor(bias_rows[0:32, lo:hi], rest[0:32], bias_rows[0:32, lo:hi], ALU.subtract).then_inc(bias_step, 1)

        @block.sync
        def _(sp):
            def load(dst, src, s):
                sp.dma_start(dst, src).then_inc(s, 16)

            load(wall[:, LX:LX + 4 * D], t_in["L0_cond_Wx"], lstm_wx_in)
            load(wall[:, LH:LH + 4 * D], t_in["L0_cond_Wh"], lstm_wh_in)
            for g, n in enumerate(("L0_cond2_b_r", "L0_cond2_b_z", "L0_cond2_b")):
                load(bias_in[:, (4 + g) * D:(5 + g) * D], t_in[n].partition_broadcast(GROUPS), gru_b_in)
            load(wall[:, QKV:QKV + 3 * D], t_in["L0_attn_W_qkv"], rest_w_in)
            for g, n in enumerate(("L0_cond2_U_r", "L0_cond2_U_z", "L0_cond2_U")):
                load(wall[:, GH + g * D:GH + (g + 1) * D], t_in[n], rest_w_in)
            for g, n in enumerate(("L0_cond2_W_r", "L0_cond2_W_z", "L0_cond2_W")):
                load(wall[:, GX + g * D:GX + (g + 1) * D], t_in[n], rest_w_in)
            load(lnw[:, :], t_in["L0_attn_ln_w"].partition_broadcast(R), small_in)
            load(lnb[:, :], t_in["L0_attn_ln_b"].partition_broadcast(R), small_in)
            sp.dma_start(bqk[:, :], t_in["L0_attn_b_qkv"][0:2 * D].rearrange("(k p) -> p k", p=128),
                         allow_slow_non_contiguous=True).then_inc(small_in, 16)
            load(bv[R:2 * R, :], t_in["L0_attn_b_qkv"][2 * D:3 * D].partition_broadcast(R), small_in)
            load(gate_w[:, :], t_in["L0_ffn_gate"], ffn_in)
            load(w1[:, :, :], t_in["L0_ffn_W1"].rearrange("e d h -> d e h"), ffn_in)
            load(w2[:, :, :, :], t_in["L0_ffn_W2"].rearrange("e (k p) d -> p e k d", p=128), ffn_in)
            sp.dma_start(b1[:, :, :], t_in["L0_ffn_b1"].rearrange("e (k p) -> p e k", p=128),
                         allow_slow_non_contiguous=True).then_inc(ffn_in, 16)
            load(b2[:, :], t_in["L0_ffn_b2"], ffn_in)

            def end_segment(n):
                sp.wait_ge(seg_done, 4 * (n + 1))
                sp.sem_inc(seg_clearing, 1)
                sp.sem_clear(range(seg_sems[0].num, seg_sems[-1].num + 1))
                sp.drain().then_inc(seg_go, 1)

            def save_x2(n, first, last):
                for k, (_, c) in enumerate(attentions(first, last)):
                    sp.wait_ge(x2_ready, 2 * (k + 1))
                    half = c % 2 * R
                    sp.dma_start(x2all[half:half + R, bass.ds(n + 1 + c, 1), :].rearrange("r n d -> r (n d)"),
                                 x2rows[:, :]).then_inc(x2_saved, 16)

            def slot(n):
                return x2all[:, bass.ds(n - 1, 1), :].rearrange("r n d -> r (n d)")

            save_x2(0, True, False)
            end_segment(0)
            with sp.Fori(1, NSEG) as n:
                sp.wait_ge(x2_saved, 16 * (2 * n - 1))
                sp.dma_start(acc[:, :], slot(n)).then_inc(acc_in, 16)
                save_x2(n, False, False)
                sp.wait_ge(acc_ready, 2 * (NE + 1))
                sp.dma_start(slot(n), acc[:, :]).then_inc(acc_saved, 16)
                sp.wait_ge(acc_saved, 16)
                end_segment(n)
            save_x2(NSEG, False, True)

            def store(lo, hi):
                for b in range(B):
                    sp.dma_start(out[b, lo * TILE:hi * TILE, :].rearrange("(k t) d -> t k d", t=TILE),
                                 x2all[b:128:B, lo + 1:hi + 1, :]).then_inc(stored, 16)

            store(0, NT - 2)
            sp.wait_ge(acc_ready, 2 * (NE + 1))
            store(NT - 2, NT - 1)
            sp.wait_ge(tail_acc_ready, NE + 2)
            store(NT - 1, NT)
            sp.wait_ge(stored, 16 * 3 * B)

        @block.gpsimd
        def _(pool):
            pool.memset(ident[:, :], 0.0).then_inc(pool_step, 1)
            pool.memset(batch_rows[:, :, :], 0.0).then_inc(pool_step, 1)
            pool.memset(onehot[:, :, :], 0.0).then_inc(pool_step, 1)
            pool.wait_ge(pool_step, 3)
            pool.affine_select(out=ident[:, :], in_=ident[:, :], compare_op=ALU.not_equal, fill=1.0, base=0,
                               pattern=[[-1, 128]], channel_multiplier=1).then_inc(ident_ready, 1)
            pool.affine_select(out=batch_rows[:, :, :], in_=batch_rows[:, :, :], compare_op=ALU.not_equal, fill=1.0,
                               base=0, pattern=[[0, 2 * C], [-1, B]], channel_multiplier=1).then_inc(batch_rows_ready, 1)
            for q in range(3):
                pool.affine_select(out=onehot[:, :, :], in_=onehot[:, :, :], compare_op=ALU.not_equal, fill=1.0,
                                   base=-32 * q, pattern=[[0, C], [-1, B]], channel_multiplier=1).then_inc(pool_step, 1)
                pool.wait_ge(pool_step, 4 + q)
            pool.memset(kT[:, 0:R], 0.0)
            pool.memset(vrows[0:R, :], 0.0)
            pool.memset(neghalf[:, :], -0.5)
            for x in lstm_h:
                pool.memset(x[:, :, :, :], 0.0)
            pool.memset(gru_h1[:, :, :], 0.0)
            pool.memset(gru_h2[:, :], 0.0)
            pool.memset(g_rh1[:, :, :], 0.0)
            pool.memset(gru_hf[:, FIRST, :, :], 0.0)
            pool.memset(xTparts[:, :, TOK:], 0.0)
            pool.memset(gathered[:, :, :], 0.0)
            pool.memset(x2all[:, 0, :], 0.0)
            pool.memset(gates[:, :], 0.0)
            pool.memset(euler[:, :], EULER)
            pool.memset(l_gates[:, :, :, :], 0.0)
            pool.memset(condT3[:, :, :], 0.0)
            pool.memset(l_c[:, :, :], 0.0)
            pool.memset(l_g[:, :, :], 0.0)
            pool.memset(g_add[:, :, :], 0.0).then_inc(pool_step, 1)
            pool.wait_ge(pool_step, 7)
            pool.memset(lstm_h[0][:, :, :, 0], -HSCALE)
            pool.memset(g_rh1[:, :, 1], -1.0)
            pool.memset(g_add[:, :, 4], GRID)
            pool.memset(g_add[:, :, 5], -GRID)
            pool.memset(g_add[:, :, 1], HSCALE).then_inc(consts_ready, 1)
            pool.wait_ge(consts_ready, 1)

            pool.wait_ge(mask_same, 1)
            pool.affine_select(out=mask[0:R, :], in_=mask[0:R, :], compare_op=ALU.is_gt, fill=0.0, base=0,
                               pattern=[[-1, R]], channel_multiplier=1).then_inc(mask_ready, 1)
            pool.affine_select(out=mask[R:2 * R, :], in_=mask[R:2 * R, :], compare_op=ALU.is_ge, fill=0.0, base=0,
                               pattern=[[1, R]], channel_multiplier=-1).then_inc(mask_ready, 1)

            def segment(n, first, last):
                seg_begin(pool, n, first)
                atts = attentions(first, last)

                def residual(k):
                    if k:
                        pool.wait_ge(x2_ready, 2 * k)
                    pool.tensor_tensor(xln[:, :], xrows[:, bass.ds(2 * n + atts[k][1], 1), :].rearrange("r n d -> r (n d)"),
                                       lnb[:, :], ALU.add).then_inc(xln_ready, 1)
                    pool.wait_ge(xln_ready, k + 1)

                def next_inputs(k):
                    if k:
                        pool.wait_ge(lstm_in_used, k)
                    pool.tensor_copy(xchunk[:, :, :], xTparts[:, :, bass.ds((2 * n + 1 + k) * R, R)]).then_inc(xchunk_ready, 1)

                def inv_std(k):
                    pool.wait_ge(ln_step, 3 * k + 2)
                    pool.tensor_scalar(var_eps[:, :], aggr[:, 1:2], LN_EPS, None, ALU.add).then_inc(var_ready, 1)
                    pool.wait_ge(var_ready, k + 1)
                    pool.tensor_tensor(rstd[:, :], var_eps[:, :], neghalf[:, :], ALU.pow).then_inc(rstd_ready, 1)
                    pool.wait_ge(rstd_ready, k + 1)

                def gather(lo, hi, step):
                    pool.tensor_copy(gathered[:, step:step + hi - lo, :], gru_hf[:, lo + 1:hi + 1, :, 3]).then_inc(gathering, 1)

                if not first:
                    pool.tensor_copy(tile_h[:, :], gathered[:, :, :].rearrange("p t b -> p (t b)")).then_inc(tile_moved, 1)
                    pool.wait_ge(tile_moved, 1)
                    gather(FIRST, SEG, 0)
                if not last:
                    next_inputs(0)
                if first:
                    pool.wait_ge(vz_ready, 1)
                    bias_parts(pool, bias_sum[:, :], 4 * D, 7 * D, 4)
                    pool.wait_ge(bias_step, 8)
                    pool.wait_ge(small_in, 16 * SMALL)
                residual(0)
                if first:
                    next_inputs(1)
                inv_std(0)
                if not first and not last:
                    next_inputs(1)
                if not first:
                    pool.wait_ge(gru_hf_ready, C)
                    gather(0, C, SEG - FIRST)
                    if not last:
                        residual(1)
                        inv_std(1)
                    pool.wait_ge(gru_hf_ready, C + LAG)
                    gather(C, C + LAG, SEG - LAG)
                if not first and not last:
                    pool.wait_ge(gate_step, 3)
                    pool.tensor_tensor(exps[:, :], euler[:, :], expo[:, :], ALU.pow).then_inc(exps_ready, 1)
                if not last:
                    seg_end(pool)

            pool.wait_ge(x_in, 16 * B)
            pool.wait_ge(mask_ready, 2)
            pool.wait_ge(small_in, 16 * SMALL)
            pool.wait_ge(setup_step, 4)
            pool.wait_ge(first_pre, 1)
            segment(0, True, False)
            with pool.Fori(1, NSEG) as n:
                segment(n, False, False)
            segment(NSEG, False, True)
            pool.wait_ge(tail_gate_step, 3)
            pool.tensor_tensor(exps[:, :], euler[:, :], expo[:, :], ALU.pow).then_inc(tail_exps_ready, 1)

        @block.scalar
        def _(act):
            for b in range(B):
                act.dma_start(xrows[b:R:B, :, :], t_in["x"][b].rearrange("(n t) d -> t n d", t=C)).then_inc(x_in, 16)
            act.dma_start(bias_in[:, 0:4 * D], t_in["L0_cond_b"].partition_broadcast(GROUPS)).then_inc(lstm_b_in, 16)
            act.dma_start(condT[:, :], t_in["cond_1024"].rearrange("b d -> d b"),
                          allow_slow_non_contiguous=True).then_inc(cond_in, 16)
            for g, n in enumerate(("L0_cond2_C_r", "L0_cond2_C_z", "L0_cond2_C")):
                act.dma_start(cw[:, g * D:(g + 1) * D], t_in[n]).then_inc(cond_in, 16)
            def query(k):
                act.wait_ge(q_pre_ready, k)
                act.activation(qT[:, :], p_a[:, 0:R], ACT.Identity, bias=bqk[:, 0:1]).then_inc(q_ready, 1)

            def move_keys(k):
                act.wait_ge(s_pre_ready, k)
                act.activation(kT[:, 0:R], kT[:, R:2 * R], ACT.Copy).then_inc(keys_moved, 1)

            def move_values(k):
                act.wait_ge(o_ready, k)
                act.activation(vrows[0:R, :], vrows[R:2 * R, :], ACT.Copy).then_inc(values_moved, 1)

            side = {1: query, 4: move_keys, 5: move_values}

            def relu(e, j, last):
                act.wait_ge(hid_pre, KH * e + j + 1)
                act.activation(hidden[:, j, :], expert_banks(last)[0][:, 0:128], ACT.Relu, bias=b1[:, e, j:j + 1],
                               scale=1.0 / HSCALE).then_inc(hid_ready, 1)

            def segment(n, first, last):
                seg_begin(act, n, first)
                steps = gru_steps(first, last)
                starts = [a for a, _ in attentions(first, last)]
                work = expert_work(first, last)
                for i in range(C + LAG if last else SEG):
                    if first and i == C:
                        act.wait_ge(small_in, 16 * SMALL)
                    if i in steps:
                        s = i - steps[0] + 1
                        c, t = gru_place(i)
                        act.wait_ge(gru_r_pre_ready, s)
                        act.activation(r_out[c], r_pre[c][:, t, :], ACT.Sigmoid).then_inc(gru_r_ready, 1)
                        act.activation(gru_hf[:, before(i), :, 2], r_pre[c][:, t, :], ACT.Sigmoid).then_inc(gru_r_again_ready, 1)
                        act.wait_ge(gru_z_pre_ready, s)
                        act.activation(g_zc[:, :], zc_pre[c][:, t, 0, :], ACT.Sigmoid, scale=-1.0).then_inc(gru_zc_ready, 1)
                        act.activation(g_mul[c][:, :, 2], zc_pre[c][:, t, 0, :], ACT.Sigmoid).then_inc(gru_z_ready, 1)
                    for k, a in enumerate(starts):
                        if i - a in side:
                            side[i - a](k + 1)
                    what, e, j = work.get(i - 1, ("", 0, 0))
                    if what == "hidden":
                        relu(e, j, last)
                    if not last:
                        c, t = lstm_place(i)
                        j = 3 * B * t
                        act.wait_ge(lstm_ifo_pre_ready, i + 1)
                        act.activation(l_gates[:, :, :, 0].rearrange("p g b -> p (g b)"), p_lstm[c][:, j:j + 3 * B], ACT.Sigmoid).then_inc(lstm_sig_ready, 1)
                        act.wait_ge(lstm_g_pre_ready, i + 1)
                        act.activation(l_g[:, :, 1], g_pre[c][:, t, :], ACT.Tanh).then_inc(lstm_g_ready, 1)
                    if i in steps:
                        c, t = gru_place(i)
                        act.wait_ge(gru_c_pre_ready, s)
                        act.activation(g_mul[c][:, :, 3], zc_pre[c][:, t, 1, :], ACT.Tanh).then_inc(gru_t_ready, 1)
                    if not last:
                        act.wait_ge(lstm_c_ready, i + 1)
                        act.activation(l_gates[:, 2, :, 1], l_c[:, :, 1], ACT.Tanh).then_inc(lstm_tc_ready, 1)
                if not last:
                    seg_end(act)

            act.wait_ge(consts_ready, 1)
            act.activation(warm[:, :], neghalf[0:1, :], ACT.Sigmoid)
            act.wait_ge(cond_in, 16 * 4)
            for q in range(3):
                ins = act.activation(condT3[:, q, 0:B], condT[:, :], ACT.Copy)
            ins.then_inc(cond3_ready, 1)
            segment(0, True, False)
            act.wait_ge(ffn_in, 16 * 5)
            with act.Fori(1, NSEG) as n:
                segment(n, False, False)
            segment(NSEG, False, True)

            for i in range(KH * NE):
                act.wait_ge(tail_hid_pre, i + 1)
                act.activation(tail_hidden[:, i // KH, i % KH, :], tail_banks[i % 4][:, 0:128], ACT.Relu,
                               bias=b1[:, i // KH, i % KH:i % KH + 1], scale=1.0 / HSCALE).then_inc(tail_hid_ready, 1)

        @block.vector
        def _(dve):
            def link(ins, n=[0]):
                n[0] += 1
                ins.then_inc(dve_step, 1)
                dve.wait_ge(dve_step, n[0])

            def split3(parts, src, rest, scale=None):
                if scale is None:
                    link(dve.tensor_copy(parts[0], src))
                    link(dve.tensor_tensor(rest, src, parts[0], ALU.subtract))
                else:
                    link(dve.tensor_scalar(parts[0], src, scale, None, ALU.mult))
                    link(dve.scalar_tensor_tensor(out=rest, in0=src, scalar=scale, in1=parts[0],
                                                  op0=ALU.mult, op1=ALU.subtract))
                link(dve.tensor_copy(parts[1], rest))
                return dve.tensor_tensor(parts[2], rest, parts[1], ALU.subtract)

            def split_w(lo, hi, scale=None):
                return split3([wparts[:, p, lo:hi] for p in range(3)], wall[:, lo:hi], wrest[:, lo:hi], scale)

            dve.memset(bias_rows[:, :], 0.0).then_inc(bias_rows_zero, 1)
            link(dve.memset(top[:, :], -1.0))
            dve.wait_ge(lstm_wx_in, 16)
            split_w(LX, LX + 4 * D).then_inc(lstm_w_ready, 1)
            dve.wait_ge(lstm_b_in, 16)
            dve.wait_ge(bias_rows_zero, 1)
            bias_parts(dve, bias_in[:, 0:4 * D], 0, 4 * D, 0)
            dve.wait_ge(xT_pre, HALF // R)
            xp = [xchunk[:, p, :] for p in range(3)]
            split3(xp, xT_bank[0][:, 0:R], xrest[:, 0:R]).then_inc(xchunk_first, 1)
            dve.wait_ge(lstm_wh_in, 16)
            split_w(LH, LH + 4 * D, 1.0 / HSCALE).then_inc(lstm_w_ready, 1)
            dve.wait_ge(same_pre, 1)
            dve.tensor_scalar(mask[:, :], p_same[:, 0:R], SCORE_SCALE, None, ALU.mult).then_inc(mask_same, 1)
            for x in g_mul:
                link(dve.memset(x, 0.0))
                link(dve.memset(x[:, :, 4:6], 1.0))
            dve.wait_ge(consts_ready, 1)

            def split_later(parts, src, rest, scale=1.0):
                return [lambda: dve.tensor_scalar(parts[0], src, scale, None, ALU.mult),
                        lambda: dve.scalar_tensor_tensor(out=rest, in0=src, scalar=scale, in1=parts[0],
                                                         op0=ALU.mult, op1=ALU.subtract),
                        lambda: dve.tensor_copy(parts[1], rest),
                        lambda: dve.tensor_tensor(parts[2], rest, parts[1], ALU.subtract)]

            later = []
            for h in range(TOK // HALF):
                later += split_later([xTparts[:, p, h * HALF:(h + 1) * HALF] for p in range(3)], xT_bank[h][:, :],
                                     xrest[:, h * HALF:(h + 1) * HALF])
            for lo, scale in ((QKV, 1.0 / HSCALE), (GH, 1.0 / HSCALE), (GX, 1.0)):
                later += split_later([wparts[:, p, lo:lo + 3 * D] for p in range(3)], wall[:, lo:lo + 3 * D],
                                     wrest[:, lo:lo + 3 * D], scale)
            later += [lambda: dve.tensor_scalar(wneg[:, :, :], wparts[:, 0:2, GH:GH + 2 * D], -1.0, None, ALU.mult)]
            assert len(later) == SETUP_LATER <= C

            def setup_later(i):
                if i == 0:
                    dve.wait_ge(xT_pre, NCH)
                elif i == 2 * 4:
                    dve.wait_ge(rest_w_in, 16 * 7)
                if i:
                    dve.wait_ge(setup_step, i)
                later[i]().then_inc(setup_step, 1)

            def scan(out_, mul, op, other):
                def flat(x):
                    return x.rearrange("p b k -> p (b k)")
                return dve.tensor_tensor_scan(flat(out_), flat(mul), flat(other), 0.0, ALU.mult, op)

            def gru_gates(i, s):
                was = gru_hf[:, before(i), :, :]
                dve.wait_ge(gru_r_ready, s)
                dve.tensor_tensor(g_rh1[:, :, 3], r_out[gru_place(i)[0]], was[:, :, 3], ALU.mult).then_inc(gru_rh1_ready, 1)
                dve.wait_ge(gru_rh1_ready, s)
                dve.wait_ge(gru_r_again_ready, s)
                scan(g_rh2[:, :, :], was, ALU.subtract, g_rh1[:, :, :]).then_inc(gru_rh2_ready, 1)
                dve.wait_ge(gru_zc_ready, s)
                dve.tensor_tensor(g_add[:, :, 3], g_zc[:, :], was[:, :, 3], ALU.mult).then_inc(gru_kept_ready, 1)

            def gru_state(i, s, kept, last):
                now = gru_hf[:, i + 1, :, :]
                dve.wait_ge(gru_t_ready, s)
                if kept and i == FIRST:
                    dve.wait_ge(gathering, 1)
                if last:
                    dve.wait_ge(gru_kept_ready, s)
                scan(now, g_mul[gru_place(i)[0]], ALU.add, g_add[:, :, :]).then_inc(gru_hf_ready, 1)
                scan(gru_h1[:, :, :], g_mul[gru_place(i)[0]], ALU.add, g_add[:, :, :]).then_inc(gru_h1_ready, 1)
                dve.wait_ge(gru_hf_ready, s)
                dve.scalar_tensor_tensor(out=gru_h2[:, :], in0=now[:, :, 4], scalar=GRID, in1=now[:, :, 3],
                                         op0=ALU.subtract, op1=ALU.subtract).then_inc(gru_h2_ready, 1)

            def lstm_cell(i):
                dve.wait_ge(lstm_sig_ready, i + 1)
                dve.tensor_tensor(l_gates[:, 0, :, 1], l_gates[:, 1, :, 0], l_c[:, :, 1], ALU.mult).then_inc(lstm_fc_ready, 1)
                dve.wait_ge(lstm_fc_ready, i + 1)
                dve.wait_ge(lstm_g_ready, i + 1)
                scan(l_c[:, :, :], l_g[:, :, :], ALU.add, l_gates[:, 0, :, :]).then_inc(lstm_c_ready, 1)

            l_out = l_gates[:, :, :, :].rearrange("p g b k -> p (g b k)")[:, 2 * 3 * B - 1:3 * 3 * B - 1]

            def lstm_state(i):
                dve.wait_ge(lstm_tc_ready, i + 1)
                dve.scalar_tensor_tensor(out=lstm_h[0][:, i + 1, :, 2], in0=l_gates[:, 2, :, 0], scalar=HSCALE,
                                         in1=l_gates[:, 2, :, 1], op0=ALU.mult, op1=ALU.mult).then_inc(lstm_h1_ready, 1)
                dve.wait_ge(lstm_h1_ready, i + 1)
                dve.tensor_tensor_scan(lstm_h[1][:, i + 1, :, :].rearrange("p b k -> p (b k)"), l_out,
                                       lstm_h[0][:, i + 1, :, :].rearrange("p b k -> p (b k)"), 0.0,
                                       ALU.mult, ALU.subtract).then_inc(lstm_h2_ready, 1)

            def keys(k, saved):
                if k > 1:
                    dve.wait_ge(keys_moved, k - 1)
                dve.wait_ge(k_pre_ready, k)
                dve.tensor_scalar(kT[:, R:2 * R], p_b[:, 0:R], bqk[:, 1:2], None, ALU.add).then_inc(k_ready, 1)

            def values(k, saved):
                if k > 1:
                    dve.wait_ge(values_moved, k - 1)
                dve.wait_ge(v_pre_ready, k)
                dve.tensor_tensor(vrows[R:2 * R, :], p_a[R:2 * R, 0:D], bv[R:2 * R, :], ALU.add).then_inc(v_ready, 1)

            def masked_scores(k, saved):
                dve.wait_ge(s_pre_ready, k)
                dve.tensor_tensor(sT[:, :], p_b[:, 0:R], mask[:, :], ALU.mult).then_inc(s_ready, 1)

            def ln_stats(k, saved):
                dve.wait_ge(o_ready, k)
                dve.bn_stats(stats[:, :], p_b[0:R, 0:D]).then_inc(ln_step, 1)

            def ln_variance(k, saved):
                dve.wait_ge(ln_step, 3 * k - 2)
                dve.bn_aggr(aggr[:, :], stats[:, :]).then_inc(ln_step, 1)

            def ln_centre(k, saved):
                dve.wait_ge(ln_step, 3 * k - 1)
                dve.scalar_tensor_tensor(out=centred[:, :], in0=p_b[0:R, 0:D], scalar=aggr[:, 0:1], in1=lnw[:, :],
                                         op0=ALU.subtract, op1=ALU.mult).then_inc(ln_step, 1)

            def residual(k, saved):
                dve.wait_ge(ln_step, 3 * k)
                dve.wait_ge(rstd_ready, k)
                dve.wait_ge(xln_ready, k)
                if saved is not None:
                    dve.wait_ge(x2_saved, saved)
                residual_half(slice(0, D // 2))

            def residual_rest(k, saved):
                residual_half(slice(D // 2, D))

            def residual_half(cols):
                dve.scalar_tensor_tensor(out=x2rows[:, cols], in0=centred[:, cols], scalar=rstd[:, 0:1], in1=xln[:, cols],
                                         op0=ALU.mult, op1=ALU.add).then_inc(x2_ready, 1)

            def split_a(k, saved):
                dve.wait_ge(x2T_ready, k)
                dve.tensor_copy(x2parts[0][:, :], p_a[:, 0:R]).then_inc(x2p_ready, 1)

            def split_b(k, saved):
                dve.wait_ge(x2p_ready, 3 * k - 2)
                dve.tensor_tensor(x2rest[:, :], p_a[:, 0:R], x2parts[0][:, :], ALU.subtract).then_inc(x2_split, 1)

            def split_c(k, saved):
                dve.wait_ge(x2_split, k)
                dve.tensor_copy(x2parts[1][:, :], x2rest[:, :]).then_inc(x2p_ready, 1)

            def split_d(k, saved):
                dve.wait_ge(x2p_ready, 3 * k - 1)
                dve.tensor_tensor(x2parts[2][:, :], x2rest[:, :], x2parts[1][:, :], ALU.subtract).then_inc(x2p_ready, 1)

            side = {1: [keys], 2: [values], 3: [masked_scores], 4: [ln_stats], 5: [ln_centre], 6: [residual],
                    7: [split_a], 8: [split_c]}
            side_middle = {4: [ln_variance], 6: [residual_rest], 7: [split_b], 8: [split_d]}

            def gate_operations(bank):
                return [
                    lambda: dve.tensor_copy(logits[:, :], bank[:, 0:NE]),
                    lambda: dve.max(largest[:, :], logits[:, :]),
                    lambda: dve.tensor_scalar(expo[:, :], logits[:, :], largest[:, 0:1], 1.0 / HSCALE,
                                              ALU.subtract, ALU.mult),
                    lambda: dve.tensor_reduce(row_sum[:, :], exps[:, :], AX.X, ALU.add),
                    lambda: dve.reciprocal(row_inv[:, :], row_sum[:, :]),
                    lambda: dve.tensor_scalar(probs[:, :], exps[:, :], row_inv[:, 0:1], None, ALU.mult),
                    lambda: dve.max(largest[:, :], probs[:, :]),
                    lambda: dve.tensor_copy(top[:, 0:2], largest[:, 0:2]),
                    lambda: dve.match_replace(struck[:, :], top[:, :], probs[:, :], -2.0),
                    lambda: dve.scalar_tensor_tensor(out=chosen[:, :], in0=struck[:, :], scalar=0.0, in1=probs[:, :],
                                                     op0=ALU.is_lt, op1=ALU.mult),
                    lambda: dve.tensor_reduce(row_sum[:, :], chosen[:, :], AX.X, ALU.add),
                    lambda: dve.tensor_scalar(row_sum[:, :], row_sum[:, :], 1e-12, None, ALU.max),
                    lambda: dve.reciprocal(row_inv[:, :], row_sum[:, :]),
                    lambda: dve.tensor_scalar(gates[:, :], chosen[:, :], row_inv[:, 0:1], None, ALU.mult),
                ]

            gate_ops = gate_operations(p_a)

            def next_gates(j):
                if j == 0:
                    dve.wait_ge(logits_ready, 1)
                elif j == 3:
                    dve.wait_ge(exps_ready, 1)
                else:
                    dve.wait_ge(gate_step, j)
                gate_ops[j]().then_inc(gate_step, 1)

            HALVES = [slice(0, D // 2), slice(D // 2, D)]

            def expert_sums(what, e, j, last, half):
                bank_h, bank_e = expert_banks(last)
                total = x2all[:, NT - 1, :] if last else acc[:, :]
                cols = HALVES[half]
                if what == "gates" and half == 0:
                    dve.wait_ge(gT_pre, 1)
                    dve.tensor_copy(gates_T[:, :], bank_h[0:NE, 0:128]).then_inc(gT_ready, 1)
                elif what == "bias":
                    dve.wait_ge(eo_pre, 1)
                    if last:
                        dve.wait_ge(x2_saved, 16 * (NCH - 1))
                    else:
                        dve.wait_ge(acc_in, 16)
                    dve.tensor_tensor(total[:, cols], bank_e[:, cols], total[:, cols], ALU.add).then_inc(acc_ready, 1)
                elif what == "out" and j == KH - 1:
                    if half == 0:
                        dve.wait_ge(eo_pre, e + 2)
                    dve.wait_ge(acc_ready, 2 * (e + 1) + half)
                    dve.scalar_tensor_tensor(out=total[:, cols], in0=bank_e[:, cols], scalar=gates[:, e:e + 1],
                                             in1=total[:, cols], op0=ALU.mult, op1=ALU.add).then_inc(acc_ready, 1)

            def segment(n, first, last):
                seg_begin(dve, n, first)
                steps = gru_steps(first, last)
                atts = attentions(first, last)
                kept = not first
                work = expert_work(first, last)
                for i in range(C + LAG if last else SEG):
                    if first and i < len(later):
                        setup_later(i)
                    if first and i == 1:
                        dve.wait_ge(vz_pre, 1)
                        dve.wait_ge(gru_b_in, 16 * 3)
                        dve.tensor_tensor(bias_sum[:, :], p_vz[0:GROUPS, 0:3 * D], bias_in[:, 4 * D:7 * D],
                                          ALU.add).then_inc(vz_ready, 1)
                    if first and i == C:
                        dve.wait_ge(mask_ready, 2)
                        dve.wait_ge(small_in, 16 * SMALL)
                    for k, (a, c) in enumerate(atts):
                        for piece in side.get(i - a, []):
                            piece(k + 1, None if first else 16 * (2 * n + c))
                    if i - 1 in work:
                        expert_sums(*work[i - 1], last, 0)
                    if not first and not last and i in GATE_STEPS:
                        next_gates(GATE_STEPS[i])
                    if i in steps:
                        gru_gates(i, i - steps[0] + 1)
                    for k, (a, c) in enumerate(atts):
                        for piece in side_middle.get(i - a, []):
                            piece(k + 1, None if first else 16 * (2 * n + c))
                    if i - 1 in work:
                        expert_sums(*work[i - 1], last, 1)
                    if not last:
                        lstm_cell(i)
                    if i in steps:
                        gru_state(i, i - steps[0] + 1, kept, last)
                    if not last:
                        lstm_state(i)
                if not last:
                    seg_end(dve)

            segment(0, True, False)
            with dve.Fori(1, NSEG) as n:
                segment(n, False, False)
            segment(NSEG, False, True)

            dve.wait_ge(tail_logits_ready, 1)
            for j, operation in enumerate(gate_operations(p_b)):
                if j == 3:
                    dve.wait_ge(tail_exps_ready, 1)
                elif j:
                    dve.wait_ge(tail_gate_step, j)
                operation().then_inc(tail_gate_step, 1)
            dve.wait_ge(tail_gT_pre, 1)
            dve.tensor_copy(gates_T[:, :], p_a[0:NE, 0:128]).then_inc(tail_gT_ready, 1)
            dve.wait_ge(x2_saved, 16 * NCH)
            last_tile = x2all[:, NT, :]
            sums = [last_tile, acc[:, :]]

            def tail_add(e, n):
                dve.wait_ge(tail_eo_pre, tail_out_complete(e))
                if n:
                    dve.wait_ge(tail_acc_ready, n)
                dve.scalar_tensor_tensor(out=sums[e % 2], in0=tail_out(e), scalar=gates[:, e:e + 1], in1=sums[e % 2],
                                         op0=ALU.mult, op1=ALU.add).then_inc(tail_acc_ready, 1)

            dve.wait_ge(tail_gate_step, 14)
            tail_add(0, 0)
            dve.tensor_scalar(sums[1], tail_out(1), gates[:, 1:2], None, ALU.mult).then_inc(tail_acc_ready, 1)
            tail_add(2, 1)
            tail_add(3, 2)
            dve.wait_ge(tail_bias_pre, 1)
            dve.wait_ge(tail_acc_ready, 4)
            dve.tensor_tensor(sums[1], p_a[:, 0:D], sums[1], ALU.add).then_inc(tail_acc_ready, 1)
            tail_add(4, 3)
            tail_add(5, 5)
            tail_add(6, 6)
            dve.wait_ge(tail_acc_ready, 8)
            dve.tensor_tensor(sums[1], sums[0], sums[1], ALU.add).then_inc(tail_acc_ready, 1)
            dve.wait_ge(tail_eo_pre, NE)
            dve.wait_ge(tail_acc_ready, 9)
            dve.scalar_tensor_tensor(out=last_tile, in0=tail_out(NE - 1), scalar=gates[:, NE - 1:NE], in1=sums[1],
                                     op0=ALU.mult, op1=ALU.add).then_inc(tail_acc_ready, 1)

        @block.tensor
        def _(pe):
            def mm(out_, lhsT, rhs, start=False):
                return pe.matmul(out_, lhsT, rhs, start=start, stop=True, skip_group_check=True)

            def by_step(x):
                return x.rearrange("p (t b) -> p t b", b=B)

            def lstm_bias(c, g):
                mm(lstm_pre(c, g), bias_rows[:, g * D:(g + 1) * D], onehot[:, :, :], start=(g in (3, 0)))

            def lstm_from_x(c, g):
                for a, b in PROD_X:
                    ins = mm(lstm_pre(c, g), w(a, LX + g * D), by_step(xchunk[:, b, :]))
                return ins

            def gru_outs(c):
                return [r_pre[c], zc_pre[c][:, :, 0, :], zc_pre[c][:, :, 1, :]]

            pe.wait_ge(ident_ready, 1)
            pe.wait_ge(x_in, 16 * B)
            for n in range(NCH):
                h, j = n * R // HALF, n * R % HALF
                pe.transpose(xT_bank[h][:, j:j + R], xrows[:, n, :], ident[0:R, 0:R]).then_inc(xT_pre, 1)
            pe.wait_ge(batch_rows_ready, 1)
            batches = batch_rows[:, :, :].rearrange("p t b -> p (t b)")
            mm(p_same[:, 0:R], batches, batches[:, 0:R], start=True).then_inc(same_pre, 1)
            pe.wait_ge(bias_step, 4)
            pe.wait_ge(consts_ready, 1)
            for g in (3, 0, 1, 2):
                lstm_bias(0, g)
            pe.wait_ge(cond_in, 16 * 4)
            pe.wait_ge(lstm_wh_in, 16)
            for g in range(4):
                mm(lstm_pre(0, g)[:, 0, :], wall[:, LH + g * D:LH + (g + 1) * D], condT[:, :])
            pe.wait_ge(xchunk_first, 1)
            for g in range(4):
                ins = lstm_from_x(0, g)
            ins.then_inc(first_pre, 1)
            pe.wait_ge(lstm_w_ready, 2)

            def lstm_products(i, gates, pairs):
                c, t = lstm_place(i)
                for g in gates:
                    for a, b in pairs:
                        ins = mm(lstm_pre(c, g)[:, t, :], w(a, LH + g * D), lstm_h[b][:, before(i), :, 2])
                return ins

            def gru_products(i, g, pairs):
                c, t = gru_place(i)
                h = [gru_h1[:, :, 5], gru_h2[:, :]] if g < 2 else [g_rh1[:, :, 3], g_rh2[:, :, 3]]
                for a, b in pairs:
                    weight = wneg[:, a, g * D:(g + 1) * D] if g < 2 and b == 1 else w(a, GH + g * D)
                    ins = mm(gru_outs(c)[g][:, t, :], weight, h[b])
                return ins

            pairs = PROD_FIRST + PROD_SECOND

            def states(c):
                lo = 1 if c == 0 else 1 + C
                return [lstm_h[p][:, lo:lo + C, :, 2].rearrange("p t b -> p (t b)") for p in range(PARTS_H)]

            def queries_keys(k, c, last):
                if k == 2:
                    pe.wait_ge(hid_ready, sum(1 for i, x in expert_work(False, False).items() if i < C and x[0] == "hidden"))
                    pe.wait_ge(acc_ready, 2 + 2 * sum(1 for i, x in expert_work(False, False).items()
                                                      if i < C and x[0] == "out" and x[2] == KH - 1))
                for j, (out_, done) in enumerate(((p_a, q_pre_ready), (p_b, k_pre_ready))):
                    for m, (a, b) in enumerate(pairs):
                        ins = mm(out_[:, 0:R], w(a, QKV + j * D), states(c)[b], start=(m == 0))
                    ins.then_inc(done, 1)

            def values(k, c, last):
                pe.wait_ge(q_ready, k)
                for m, (a, b) in enumerate(pairs):
                    ins = mm(p_a[R:2 * R, 0:D], states(c)[b], w(a, QKV + 2 * D), start=(m == 0))
                ins.then_inc(v_pre_ready, 1)

            def scores(k, c, last):
                pe.wait_ge(k_ready, k)
                mm(p_b[:, 0:R], kT[:, :], qT[:, :], start=True).then_inc(s_pre_ready, 1)

            def output(k, c, last):
                pe.wait_ge(s_ready, k)
                pe.wait_ge(v_ready, k)
                mm(p_b[0:R, 0:D], sT[:, :], vrows[:, :], start=True).then_inc(o_ready, 1)

            def columns(k, c, last):
                pe.wait_ge(x2_ready, 2 * k)
                pe.transpose(p_a[:, 0:R], x2rows[:, :], ident[0:R, 0:R]).then_inc(x2T_ready, 1)

            def gru_from_x(part):
                def piece(k, c, last):
                    outs = gru_outs(c % 2)
                    if part == 0:
                        for g in range(3):
                            mm(outs[g], bias_rows[:, (4 + g) * D:(5 + g) * D], onehot[:, :, :],
                               start=(g == 1 or g == 0 and last))
                    pe.wait_ge(x2p_ready, 3 * (k - 1) + part + 1)
                    for g in range(3):
                        for a in range(3 - part):
                            mm(outs[g], w(a, GX + g * D), by_step(x2parts[part][:, :]))
                return piece

            side = {0: [queries_keys], 1: [values], 2: [scores], 3: [output], 6: [columns], 7: [gru_from_x(0)],
                    8: [gru_from_x(1), gru_from_x(2)]}
            AHEAD = {4: 3, 5: 0, 6: 1, 9: 2}

            def experts(what, e, j, last, logits_before):
                bank_h, bank_e = expert_banks(last)
                if what == "gates":
                    pe.transpose(bank_h[0:NE, 0:128], gates[:, :], ident[:, :]).then_inc(gT_pre, 1)
                elif what == "bias":
                    pe.wait_ge(gT_ready, 1)
                    mm(bank_e[:, 0:D], gates_T[:, :], b2[:, :], start=True).then_inc(eo_pre, 1)
                elif what == "hidden":
                    if e or j:
                        pe.wait_ge(hid_ready, KH * e + j)
                    else:
                        pe.wait_ge(tile_moved, 1)
                    if logits_before:
                        pe.wait_ge(gate_step, 1)
                    mm(bank_h[:, 0:128], w1[:, e, j * 128:(j + 1) * 128], tile_h[:, :], start=True).then_inc(hid_pre, 1)
                elif what == "out":
                    if j == 0:
                        pe.wait_ge(hid_ready, KH * (e + 1))
                        pe.wait_ge(acc_ready, 2 * (e + 1))
                    ins = mm(bank_e[:, 0:D], hidden[:, j, :], w2[:, e, j, :], start=(j == 0))
                    if j == KH - 1:
                        ins.then_inc(eo_pre, 1)

            def segment(n, first, last):
                seg_begin(pe, n, first)
                steps = gru_steps(first, last)
                atts = attentions(first, last)
                work = expert_work(first, last)
                for i in range(C + LAG if last else SEG):
                    if first and i == C:
                        pe.wait_ge(setup_step, SETUP_LATER)
                        pe.wait_ge(bias_step, 8)
                    s = i - steps[0]
                    if i in steps:
                        if s:
                            pe.wait_ge(gru_h1_ready, s)
                        gru_products(i, 0, PROD_FIRST)
                        if s:
                            pe.wait_ge(gru_h2_ready, s)
                        gru_products(i, 0, PROD_SECOND).then_inc(gru_r_pre_ready, 1)
                        gru_products(i, 1, PROD_FIRST + PROD_SECOND).then_inc(gru_z_pre_ready, 1)
                    if not last:
                        if i:
                            pe.wait_ge(lstm_h1_ready, i)
                        lstm_products(i, range(3), PROD_FIRST)
                        if i:
                            pe.wait_ge(lstm_h2_ready, i)
                        lstm_products(i, range(3), PROD_SECOND).then_inc(lstm_ifo_pre_ready, 1)
                        if i in steps:
                            pe.wait_ge(gru_r_again_ready, s + 1)
                        lstm_products(i, [3], PROD_FIRST + PROD_SECOND).then_inc(lstm_g_pre_ready, 1)
                    if i in steps:
                        pe.wait_ge(gru_rh1_ready, s + 1)
                        pe.wait_ge(gru_z_ready, s + 1)
                        gru_products(i, 2, PROD_FIRST)
                    if i in steps:
                        pe.wait_ge(gru_rh2_ready, s + 1)
                        gru_products(i, 2, PROD_SECOND).then_inc(gru_c_pre_ready, 1)
                    for k, (a, c) in enumerate(atts):
                        for piece in side.get(i - a, []):
                            piece(k + 1, c, last)
                    if i in work:
                        experts(*work[i], last, not last and i > LOGITS)
                    if not first and not last and i == LOGITS:
                        pe.wait_ge(gathering, 3)
                        mm(p_a[:, 0:NE], gathered[:, :, :].rearrange("p t b -> p (t b)"), gate_w[:, :],
                           start=True).then_inc(logits_ready, 1)
                    if first and i == 0:
                        pe.wait_ge(cond3_ready, 1)
                        mm(p_vz[0:GROUPS, 0:3 * D], condT3[:, :, :].rearrange("p q r -> p (q r)"), cw[:, :],
                           start=True).then_inc(vz_pre, 1)
                    if not last and i % C in AHEAD:
                        k, g = i // C + 1, AHEAD[i % C]
                        pe.wait_ge(xchunk_ready, k)
                        lstm_bias(k % 2, g)
                        ins = lstm_from_x(k % 2, g)
                        if g == 2:
                            ins.then_inc(lstm_in_used, 1)
                if not last:
                    seg_end(pe)

            segment(0, True, False)
            pe.wait_ge(ffn_in, 16 * 5)
            with pe.Fori(1, NSEG) as n:
                segment(n, False, False)
            segment(NSEG, False, True)

            rows = gathered[:, :, :].rearrange("p t b -> p (t b)")

            def tail_rows(i):
                if i >= 4:
                    pe.wait_ge(tail_hid_ready, i - 3)
                mm(tail_banks[i % 4][:, 0:128], w1[:, i // KH, i % KH * 128:(i % KH + 1) * 128], rows,
                   start=True).then_inc(tail_hid_pre, 1)

            pe.wait_ge(gathering, 3)
            mm(p_b[:, 0:NE], rows, gate_w[:, :], start=True).then_inc(tail_logits_ready, 1)

            def tail_expert(e):
                pe.wait_ge(tail_hid_ready, KH * (e + 1))
                if e == NE - 1:
                    pe.wait_ge(tail_gate_step, 1)
                for j in range(KH):
                    ins = mm(tail_out(e), tail_hidden[:, e, j, :], w2[:, e, j, :],
                             start=(j == 0 and e in (0, 4, NE - 1)))
                ins.then_inc(tail_eo_pre, 1)

            for e in range(NE):
                for j in range(KH):
                    tail_rows(KH * e + j)
                if e:
                    tail_expert(e - 1)
                if e == 4:
                    pe.wait_ge(tail_gate_step, 14)
                    pe.transpose(p_a[0:NE, 0:128], gates[:, :], ident[:, :]).then_inc(tail_gT_pre, 1)
                if e == 5:
                    pe.wait_ge(tail_gT_ready, 1)
                    mm(p_a[:, 0:D], gates_T[:, :], b2[:, :], start=True).then_inc(tail_bias_pre, 1)
            tail_expert(NE - 1)


_INS = ["x", "cond_1024", "L0_cond_Wx", "L0_cond_Wh", "L0_cond_b", "L0_attn_W_qkv", "L0_attn_b_qkv",
        "L0_attn_ln_w", "L0_attn_ln_b", "L0_cond2_W_z", "L0_cond2_U_z", "L0_cond2_C_z", "L0_cond2_b_z",
        "L0_cond2_W_r", "L0_cond2_U_r", "L0_cond2_C_r", "L0_cond2_b_r", "L0_cond2_W", "L0_cond2_U",
        "L0_cond2_C", "L0_cond2_b", "L0_ffn_gate", "L0_ffn_W1", "L0_ffn_b1", "L0_ffn_W2", "L0_ffn_b2"]


def kernel(**inputs):
    import numpy as _np
    import concourse.bacc as _bacc
    from concourse import mybir as _mybir
    from concourse.bass_utils import run_bass_kernel_spmd as _run

    nc = _bacc.Bacc("TRN2", target_bir_lowering=False, num_devices=1)
    arrays, t_in = {}, {}
    for name in _INS:
        a = _np.ascontiguousarray(inputs[name])
        arrays[f"in_{name}"] = a
        t_in[name] = nc.dram_tensor(f"in_{name}", a.shape, _mybir.dt.from_np(a.dtype), kind="ExternalInput").ap()
    out = nc.dram_tensor("out_0", inputs["x"].shape, _mybir.dt.float32, kind="ExternalOutput").ap()
    adaln_kernel(nc, t_in, out)
    r = _run(nc, [arrays], core_ids=[0])
    return r.results[0]["out_0"]
```
